# Optimizing a Trainium2 kernel written in Bass

```python
import numpy as np
import jax
import jax.numpy as jnp

def _softmax(x, axis=-1):
    return jax.nn.softmax(x, axis=axis)

def _gelu(x):
    return jax.nn.gelu(x, approximate=True)

def _silu(x):
    return jax.nn.silu(x)

def _sigmoid(x):
    return jax.nn.sigmoid(x)

def _layernorm(x, axis=-1, eps=1e-05):
    m = jnp.mean(x, axis=axis, keepdims=True)
    v = jnp.var(x, axis=axis, keepdims=True)
    return (x - m) / jnp.sqrt(v + eps)

def _scatter_add(tgt, idx, src, axis=0):
    return tgt.at[idx].add(src)

def _segment_sum(src, seg, n):
    return jax.ops.segment_sum(src, seg, n)
kernel_name = 'mk_gnn_preln_d2_gnn_r64_d3a5fb'

def setup_inputs(seed: int=0):
    np.random.seed(seed)
    _w = jnp.asarray

    def _rec_inputs():
        import jax
        import jax.numpy as jnp
        _gk = jax.random.key(seed)
        x = -0.000202 + 1 * jax.random.normal(jax.random.fold_in(_gk, 1), (100000, 128), jnp.float32)
        src = jax.random.randint(jax.random.fold_in(_gk, 2), (25000,), 0, 100000, jnp.int32)
        dst = jnp.minimum((100000 * jax.random.uniform(jax.random.fold_in(_gk, 3), (25000,)) ** 2.0).astype(jnp.int32), 99999)
        _o = jnp.argsort(dst, stable=True)
        src = src[_o]
        dst = dst[_o]
        edge_attr_32 = 0.000196303 + 1.00016 * jax.random.normal(jax.random.fold_in(_gk, 11), (25000, 32), jnp.float32)
        return (x, src, dst, edge_attr_32)
    x, src, dst, edge_attr_32 = _rec_inputs()

    def _L0_gnn_setup():
        import jax, jax.numpy as jnp
        import numpy as np
        N_NODES = 50000
        N_EDGES = 12500
        D = 128
        EDGE_DIM = 32
        BN_EPS = 1e-05

        def _batchnorm(x, gamma, beta):
            mean = jnp.mean(x, axis=0)
            var = jnp.var(x, axis=0)
            return (x - mean) * jax.lax.rsqrt(var + BN_EPS) * gamma + beta
        key = jax.random.key(seed)
        ks = jax.random.split(key, 8)
        s_e = 1.0 / np.sqrt(EDGE_DIM)
        s_d = 1.0 / np.sqrt(D)
        return {'x': jax.random.normal(ks[0], (N_NODES, D), dtype=jnp.float32), 'edge_index': jax.random.randint(ks[1], (2, N_EDGES), 0, N_NODES, dtype=jnp.int32), 'edge_attr': jax.random.normal(ks[2], (N_EDGES, EDGE_DIM), dtype=jnp.float32), 'epsilon': jnp.zeros((1,), dtype=jnp.float32), 'We': jax.random.uniform(ks[3], (EDGE_DIM, D), jnp.float32, -s_e, s_e), 'be': jnp.zeros((D,), jnp.float32), 'W1': jax.random.uniform(ks[4], (D, D), jnp.float32, -s_d, s_d), 'b1': jnp.zeros((D,), jnp.float32), 'g1': jnp.ones((D,), jnp.float32), 'beta1': jnp.zeros((D,), jnp.float32), 'W2': jax.random.uniform(ks[5], (D, D), jnp.float32, -s_d, s_d), 'b2': jnp.zeros((D,), jnp.float32), 'g2': jnp.ones((D,), jnp.float32), 'beta2': jnp.zeros((D,), jnp.float32)}
    _L0_gnn_all = _L0_gnn_setup()
    _L0_gnn_in = {k: v for k, v in _L0_gnn_all.items() if k in ('epsilon', 'We', 'be', 'W1', 'b1', 'g1', 'beta1', 'W2', 'b2', 'g2', 'beta2')}
    del _L0_gnn_all

    def _L1_gnn_setup():
        import jax, jax.numpy as jnp
        import numpy as np
        N_NODES = 50000
        N_EDGES = 9375
        IN_CH = 128
        OUT_CH = 128
        key = jax.random.key(seed)
        k1, k2, k3, k4 = jax.random.split(key, 4)
        x = jax.random.normal(k1, (N_NODES, IN_CH), dtype=jnp.float32)
        edge_index = jax.random.randint(k2, (2, N_EDGES), 0, N_NODES, dtype=jnp.int64)
        W = jax.random.normal(k3, (OUT_CH, IN_CH), dtype=jnp.float32) * (1.0 / np.sqrt(IN_CH))
        b = jax.random.normal(k4, (OUT_CH,), dtype=jnp.float32) * 0.01
        return {'x': x, 'edge_index': edge_index, 'W': W, 'b': b}
    _L1_gnn_all = _L1_gnn_setup()
    _L1_gnn_in = {k: v for k, v in _L1_gnn_all.items() if k in ('W', 'b')}
    del _L1_gnn_all
    return {'x': x, 'src': src, 'dst': dst, 'edge_attr_32': edge_attr_32, 'L0_gnn_epsilon': _L0_gnn_in['epsilon'], 'L0_gnn_We': _L0_gnn_in['We'], 'L0_gnn_be': _L0_gnn_in['be'], 'L0_gnn_W1': _L0_gnn_in['W1'], 'L0_gnn_b1': _L0_gnn_in['b1'], 'L0_gnn_g1': _L0_gnn_in['g1'], 'L0_gnn_beta1': _L0_gnn_in['beta1'], 'L0_gnn_W2': _L0_gnn_in['W2'], 'L0_gnn_b2': _L0_gnn_in['b2'], 'L0_gnn_g2': _L0_gnn_in['g2'], 'L0_gnn_beta2': _L0_gnn_in['beta2'], 'L1_gnn_W': _L1_gnn_in['W'], 'L1_gnn_b': _L1_gnn_in['b']}

def reference(x, src, dst, edge_attr_32, L0_gnn_epsilon, L0_gnn_We, L0_gnn_be, L0_gnn_W1, L0_gnn_b1, L0_gnn_g1, L0_gnn_beta1, L0_gnn_W2, L0_gnn_b2, L0_gnn_g2, L0_gnn_beta2, L1_gnn_W, L1_gnn_b):
    import jax
    import jax.numpy as jnp

    def _L0_gnn_ref(x, edge_index, edge_attr, epsilon, We, be, W1, b1, g1, beta1, W2, b2, g2, beta2):
        import jax, jax.numpy as jnp
        import numpy as np
        N_NODES = 50000
        N_EDGES = 12500
        D = 128
        EDGE_DIM = 32
        BN_EPS = 1e-05

        def _batchnorm(x, gamma, beta):
            mean = jnp.mean(x, axis=0)
            var = jnp.var(x, axis=0)
            return (x - mean) * jax.lax.rsqrt(var + BN_EPS) * gamma + beta
        src, dst = (edge_index[0], edge_index[1])
        edge_feat = jax.nn.relu(edge_attr @ We + be)
        messages = x[src] + edge_feat
        agg = jax.ops.segment_sum(messages, dst, num_segments=x.shape[0])
        h = (1.0 + epsilon) * x + agg
        h = jax.nn.relu(_batchnorm(h @ W1 + b1, g1, beta1))
        h = jax.nn.relu(_batchnorm(h @ W2 + b2, g2, beta2))
        return h

    def _L1_gnn_ref(x, edge_index, W, b):
        import jax, jax.numpy as jnp
        import numpy as np
        N_NODES = 50000
        N_EDGES = 9375
        IN_CH = 128
        OUT_CH = 128
        row, col = (edge_index[0], edge_index[1])
        n = x.shape[0]
        deg = jax.ops.segment_sum(jnp.ones_like(row, dtype=x.dtype), row, num_segments=n)
        deg_inv_sqrt = jnp.where(deg > 0, jax.lax.rsqrt(jnp.where(deg > 0, deg, 1.0)), 0.0)
        norm = deg_inv_sqrt[row] * deg_inv_sqrt[col]
        msgs = norm[:, None] * x[col]
        agg = jax.ops.segment_sum(msgs, row, num_segments=n)
        return agg @ W.T + b
    edge_index = jnp.stack([src, dst])
    h = jnp.maximum(_layernorm(x, axis=-1), 0.0)
    x = x + _L0_gnn_ref(h, edge_index, edge_attr_32, L0_gnn_epsilon, L0_gnn_We, L0_gnn_be, L0_gnn_W1, L0_gnn_b1, L0_gnn_g1, L0_gnn_beta1, L0_gnn_W2, L0_gnn_b2, L0_gnn_g2, L0_gnn_beta2)
    h = jnp.maximum(_layernorm(x, axis=-1), 0.0)
    x = x + _L1_gnn_ref(h, edge_index, L1_gnn_W, L1_gnn_b)
    return x

_drawn_inputs = setup_inputs


def setup_inputs(seed=0):
    import zlib

    import numpy as np

    out = dict(_drawn_inputs(seed))
    spreads = {'L0_gnn_be': (0.0, 0.1),
     'L0_gnn_b1': (0.0, 0.8),
     'L0_gnn_g1': (1.0, 0.2),
     'L0_gnn_beta1': (0.0, 0.1),
     'L0_gnn_b2': (0.0, 0.8),
     'L0_gnn_g2': (1.0, 0.2),
     'L0_gnn_beta2': (0.0, 0.1)}
    factors = {'L1_gnn_b': 6.874}
    for name, (base, spread) in spreads.items():
        noise = np.random.default_rng([zlib.crc32(name.encode()), seed]).standard_normal(out[name].shape)
        drawn = base * np.exp(spread * noise) if base else spread * noise
        out[name] = jnp.asarray(drawn.astype(out[name].dtype))
    for name, factor in factors.items():
        out[name] = (out[name] * factor).astype(out[name].dtype)
    return out
```

```python
import concourse.bass as bass
from concourse import mybir
from contextlib import ExitStack


def preln_gin_then_gcn(nc, x, src, dst, edge_attr, epsilon, We, be, W1, b1, g1, beta1,
                       W2, b2, g2, beta2, Wl, bl, out):
    f32, bf16, i32 = mybir.dt.float32, mybir.dt.bfloat16, mybir.dt.int32
    ALU = mybir.AluOpType
    ACT = mybir.ActivationFunctionType

    N, D = x.shape
    E, DE = edge_attr.shape
    P = 128
    J = 4
    GE = P * J
    NG = 2 * -(-E // (2 * GE))
    EFULL = E // GE
    EREST = (E - EFULL * GE) // J
    C = 8
    BN = P * C
    NB = -(-N // BN)
    TAIL = N - BN
    SEEN = ((NB - 1) * BN - TAIL) // C
    BANK = 512
    PAD = N + GE
    ROWS = out.shape[0]
    ZCH = 48
    EPS = 1e-5
    QB = 10
    QW = 1 << QB
    PW = -(-(PAD + 1) // QW)
    NE = NG // 2
    assert E - EFULL * GE > 0 and EFULL == NG - 2 and ROWS % P == 0 and ROWS > PAD and (ROWS // P * D) % ZCH == 0
    assert (E - EFULL * GE) % J == 0 and ((NB - 1) * BN - TAIL) % C == 0 and PW <= P
    ZW = ROWS // P * D // ZCH

    agg = nc.dram_tensor("agg_messages", (ROWS, D), f32, kind="Internal").ap()
    dis_tab = nc.dram_tensor("inv_sqrt_degree", (PW * QW, 1), f32, kind="Internal").ap()
    xd_c = nc.dram_tensor("x_of_dst", (NG, P, J * D), f32, kind="Internal").ap()
    ad_c = nc.dram_tensor("agg_of_dst", (NG, P, J * D), f32, kind="Internal").ap()
    x2_c = nc.dram_tensor("x2_of_dst", (NG, P, J * D), f32, kind="Internal").ap()
    y1_s = nc.dram_tensor("y1_feature_major", (NB, P, BN), f32, kind="Internal").ap()
    y2_s = nc.dram_tensor("y2_feature_major", (NB, P, BN), f32, kind="Internal").ap()

    def wait(eng, sem, value):
        if not (isinstance(value, int) and value <= 0):
            eng.wait_ge(sem, value)

    def steps(eng, n, ring, step, last):
        full = (n - last) // ring
        for u in range(ring):
            step(0, u)
        with eng.Fori(1, full) as i:
            for u in range(ring):
                step(i, u)
        for k in range(full * ring, n):
            step(k // ring, k % ring)

    def node_rows(table, k, lo=0):
        base = TAIL if isinstance(k, int) and k == NB - 1 else BN * k
        return table[bass.ds(base + lo * C, (P - lo) * C), :].rearrange("(p c) d -> p (c d)", c=C)

    def edge_rows(k):
        n = EREST * J if isinstance(k, int) and k == EFULL else GE
        return edge_attr[bass.ds(k * GE, n), :].rearrange("(p j) d -> p (j d)", j=J)

    ctx = ExitStack()
    with ctx:
        def sem(name):
            return ctx.enter_context(nc.semaphore(name))

        def sb(name, shape, dt=f32, scope=ctx):
            return scope.enter_context(nc.sbuf_tensor(name, shape, dt))

        ident = sb("ident", [P, P])
        earlier = sb("earlier", [P, GE])
        trash = sb("trash", [P, J])
        src_i = sb("src_i", [P, NG, J], i32)
        dst_i = sb("dst_i", [P, NG, J], i32)
        src_k = sb("src_k", [P, NG, J])
        dst_k = sb("dst_k", [P, NG, J])
        scat2 = sb("scat2", [P, NG, J], i32)
        WeB = sb("WeB", [P, J * D])
        beB = sb("beB", [1, J * D])
        ones = sb("ones", [1, P])
        w1 = sb("w1", [D, D])
        w2 = sb("w2", [D, D])
        wl = sb("wl", [D, D])
        wlT = sb("wlT", [D, D])
        epst = sb("epst", [P, 1])
        lneps = sb("lneps", [P, 1])
        cols = sb("cols", [P, 7])
        bn_s = sb("bn_s", [P, 2])
        bn_t = sb("bn_t", [P, 2])
        stat = sb("stat", [P, 2 * (NB - 1) + C, 6])
        psum = [ctx.enter_context(nc.psum_tensor(f"psum{n}", [P, 2 * BANK], f32)) for n in range(4)]

        params = sem("params"); indices = sem("indices"); zero_set = sem("zero_set")
        cleared = sem("cleared"); zeroed = sem("zeroed"); const = sem("const")
        keys = sem("keys"); halves = sem("halves"); wlT_ps = sem("wlT_ps")
        idx_set = sem("idx_set"); xd_got = [sem(f"xd_got{n}") for n in range(2)]
        xd_kept = [sem(f"xd_kept{n}") for n in range(2)]; pool_go = sem("pool_go")
        hot = sem("hot"); hot_used = sem("hot_used"); deg_ps = sem("deg_ps")
        deg_sb = sem("deg_sb"); deg_rt = sem("deg_rt"); dis_set = sem("dis_set"); dis_out = sem("dis_out")
        N_PARAMS = 4 + 4 + 3 + 1 + 7

        with ExitStack() as scope:
            zeros = sb("zeros", [P, ZW], f32, scope)
            xd = [sb(f"xd{n}", [P, J, D], f32, scope) for n in range(2)]
            gidx = [sb(f"gidx{n}", [P, J], i32, scope) for n in range(2)]
            iota_i = sb("iota_i", [P, QW], i32, scope)
            iota_f = sb("iota_f", [P, QW], f32, scope)
            trash_i = sb("trash_i", [P, J], i32, scope)
            key_i = sb("key_i", [P, NG * J], i32, scope)
            row_i = sb("row_i", [P, NG * J], i32, scope)
            col_i = sb("col_i", [P, NG * J], i32, scope)
            row_f = sb("row_f", [P, NG * J], f32, scope)
            col_f = sb("col_f", [P, NG * J], f32, scope)
            hot_r = [sb(f"hot_r{n}", [P, P], bf16, scope) for n in range(J)]
            hot_c = [sb(f"hot_c{n}", [P, QW], bf16, scope) for n in range(J)]
            deg = sb("deg", [P, QW], f32, scope)
            root = sb("root", [P, QW], f32, scope)
            inv = sb("inv", [P, QW], f32, scope)

            with nc.Block() as block:
                @block.sync
                def _(sp):
                    sp.wait_ge(cleared, 3)
                    for table, t in ((src, src_i), (dst, dst_i)):
                        sp.dma_start(t[:, 0:EFULL, :], table[0:EFULL * GE].rearrange(
                            "(g p j) -> p g j", p=P, j=J)).then_inc(indices, 16)
                        sp.dma_start(t[0:EREST, EFULL, :], table[EFULL * GE:E].rearrange(
                            "(p j) -> p j", j=J)).then_inc(indices, 16)
                    for j in range(J):
                        sp.dma_start(WeB[DE * j:DE * (j + 1), D * j:D * (j + 1)], We[:, :]).then_inc(params, 16)
                        sp.dma_start(beB[0:1, D * j:D * (j + 1)], be.rearrange("(a d) -> a d", a=1)).then_inc(params, 16)
                    for w, t in ((W1, w1), (W2, w2), (Wl, wl)):
                        sp.dma_start(t[:, :], w[:, :]).then_inc(params, 16)
                    sp.dma_start(epst[:, :], epsilon.rearrange("(a d) -> a d", a=1).broadcast_to((P, 1))).then_inc(params, 16)
                    for n, v in enumerate((b1, g1, beta1, b2, g2, beta2, bl)):
                        sp.dma_start(cols[:, n:n + 1], v.rearrange("(p a) -> p a", a=1)).then_inc(params, 16)
                    sp.wait_ge(zero_set, 1)
                    table = agg.rearrange("(p r) d -> p (r d)", p=P)
                    with sp.Fori(0, ZCH) as z:
                        sp.dma_start(table[:, bass.ds(z * ZW, ZW)], zeros[:, :]).then_inc(zeroed, 16)

                    def keep_xd(i, u):
                        wait(sp, xd_got[u], 16 * J * (i + 1))
                        sp.dma_start(xd_c[bass.ds(2 * i + u, 1), :, :].rearrange("a p f -> p (a f)"),
                                     xd[u][:, :, :].rearrange("p j d -> p (j d)")).then_inc(xd_kept[u], 16)
                    steps(sp, NG, 2, keep_xd, 1)
                    sp.wait_ge(dis_set, 2)
                    sp.dma_start(dis_tab.rearrange("(p q) a -> p (q a)", q=QW), inv[0:PW, :]).then_inc(dis_out, 16)
                    for u in range(2):
                        sp.wait_ge(xd_kept[u], 16 * ((NG + 1 - u) // 2))
                    sp.wait_ge(zeroed, 16 * ZCH)
                    sp.wait_ge(dis_out, 16)
                    sp.wait_ge(params, 16 * N_PARAMS)

                @block.gpsimd
                def _(pool):
                    pool.memset(src_i[:, :, :], 0).then_inc(cleared, 1)
                    pool.memset(dst_i[:, :, :], 0).then_inc(cleared, 1)
                    pool.memset(WeB[:, :], 0.0).then_inc(cleared, 1)
                    pool.memset(zeros[:, :], 0.0).then_inc(zero_set, 1)
                    pool.memset(ident[:, :], 0.0).then_inc(const, 1)
                    pool.memset(earlier[:, :], 1.0).then_inc(const, 1)
                    pool.memset(ones[:, :], 1.0).then_inc(const, 1)
                    pool.memset(lneps[:, :], EPS).then_inc(const, 1)
                    pool.iota(iota_i[:, :], pattern=[[1, QW]], base=0, channel_multiplier=0).then_inc(const, 1)
                    pool.iota(trash_i[:, :], pattern=[[P, J]], base=N, channel_multiplier=1).then_inc(const, 1)
                    pool.wait_ge(const, 6)
                    pool.affine_select(out=ident[:, :], in_=ident[:, :], compare_op=ALU.not_equal, fill=1.0,
                                       base=0, pattern=[[-1, P]], channel_multiplier=1).then_inc(const, 1)
                    pool.affine_select(out=earlier[:, GE - P:GE], in_=earlier[:, GE - P:GE], compare_op=ALU.is_gt,
                                       fill=0.0, base=0, pattern=[[-1, P]], channel_multiplier=1).then_inc(const, 1)
                    pool.tensor_copy(iota_f[:, :], iota_i[:, :]).then_inc(const, 1)
                    pool.tensor_copy(trash[:, :], trash_i[:, :]).then_inc(const, 1)
                    pool.wait_ge(indices, 64)
                    pool.tensor_copy(src_k[:, :, :], src_i[:, :, :]).then_inc(keys, 1)
                    pool.tensor_copy(dst_k[:, :, :], dst_i[:, :, :]).then_inc(keys, 1)
                    pool.wait_ge(keys, 2)
                    for t in (src_k, dst_k):
                        pool.affine_select(out=t[:, EFULL:NG, :], in_=t[:, EFULL:NG, :], compare_op=ALU.is_gt,
                                           fill=float(PAD), base=E - EFULL * GE,
                                           pattern=[[-GE, NG - EFULL], [-1, J]], channel_multiplier=-J).then_inc(keys, 1)

                    def gather_xd(i, u):
                        wait(pool, xd_kept[u], 16 * i)
                        pool.sem_inc(pool_go, 1)
                        pool.tensor_copy(gidx[u][:, :], dst_i[:, bass.ds(2 * i + u, 1), :].rearrange("p a j -> p (a j)")).then_inc(idx_set, 1)
                        wait(pool, idx_set, 2 * i + u + 1)
                        pool.sem_inc(pool_go, 1)
                        for j in range(J):
                            pool.indirect_dma_start(
                                out=xd[u][:, j, :], out_offset=None, in_=x[:, :],
                                in_offset=bass.IndirectOffsetOnAxis(ap=gidx[u][:, j:j + 1], axis=0)).then_inc(xd_got[u], 16)
                    steps(pool, NG, 2, gather_xd, 1)

                @block.vector
                def _(dve):
                    dve.wait_ge(keys, 4)
                    dve.tensor_copy(key_i[:, :], src_k[:, :, :].rearrange("p g j -> p (g j)")).then_inc(halves, 1)
                    dve.wait_ge(halves, 1)
                    dve.tensor_scalar(row_i[:, :], key_i[:, :], QB, None, ALU.logical_shift_right).then_inc(halves, 1)
                    dve.tensor_scalar(col_i[:, :], key_i[:, :], QW - 1, None, ALU.bitwise_and).then_inc(halves, 1)
                    dve.wait_ge(halves, 3)
                    dve.tensor_copy(row_f[:, :], row_i[:, :]).then_inc(halves, 1)
                    dve.tensor_copy(col_f[:, :], col_i[:, :]).then_inc(halves, 1)
                    dve.wait_ge(halves, 5)
                    dve.wait_ge(const, 10)

                    def one_hots(i, u):
                        k = J * i + u
                        wait(dve, hot_used, k - J + 1)
                        dve.tensor_scalar(hot_r[u][:, :], iota_f[:, 0:P], row_f[:, bass.ds(k, 1)], None, ALU.is_equal).then_inc(hot, 1)
                        dve.tensor_scalar(hot_c[u][:, :], iota_f[:, :], col_f[:, bass.ds(k, 1)], None, ALU.is_equal).then_inc(hot, 1)
                    steps(dve, NG * J, J, one_hots, 1)
                    dve.wait_ge(deg_ps, 1)
                    dve.tensor_scalar(deg[:, :], psum[0][:, :], 1.0, None, ALU.max).then_inc(deg_sb, 1)
                    dve.wait_ge(deg_rt, 1)
                    dve.reciprocal(inv[:, :], root[:, :]).then_inc(dis_set, 1)
                    dve.wait_ge(dis_set, 1)
                    dve.scalar_tensor_tensor(out=inv[:, :], in0=psum[0][:, :], scalar=0.0, in1=inv[:, :],
                                             op0=ALU.is_gt, op1=ALU.mult).then_inc(dis_set, 1)
                    dve.wait_ge(params, 16 * N_PARAMS)
                    dve.tensor_scalar(epst[:, :], epst[:, :], 1.0, None, ALU.add).then_inc(const, 1)
                    dve.wait_ge(wlT_ps, 1)
                    dve.tensor_copy(wlT[:, :], psum[1][:, 0:D]).then_inc(const, 1)

                @block.scalar
                def _(act):
                    act.wait_ge(deg_sb, 1)
                    act.activation(root[:, :], deg[:, :], ACT.Sqrt).then_inc(deg_rt, 1)

                @block.tensor
                def _(pe):
                    pe.wait_ge(const, 10)
                    pe.wait_ge(params, 16 * N_PARAMS)
                    nc.tensor.transpose(psum[1][:, 0:D], wl[:, :], ident[:, :]).then_inc(wlT_ps, 1)

                    def add_degrees(i, u):
                        k = J * i + u
                        first, final = isinstance(k, int) and k == 0, isinstance(k, int) and k == NG * J - 1
                        wait(pe, hot, 2 * (k + 1))
                        for h in range(QW // BANK):
                            m = nc.tensor.matmul(psum[0][:, h * BANK:(h + 1) * BANK], hot_r[u][:, :],
                                                 hot_c[u][:, h * BANK:(h + 1) * BANK], start=first, stop=final)
                        m.then_inc(hot_used, 1)
                    steps(pe, NG * J, J, add_degrees, 1)
                    pe.wait_ge(hot_used, NG * J)
                    pe.sem_inc(deg_ps, 1)

        R = 3
        ea_in = [sem(f"ea_in{n}") for n in range(R)]; xs_got = [sem(f"xs_got{n}") for n in range(R)]
        sent = [sem(f"sent{n}") for n in range(R)]
        gi_set = sem("gi_set"); own_set = sem("own_set"); go2 = sem("go2"); dve_go = sem("dve_go")
        eaT_ps = sem("eaT_ps"); eaT_sb = sem("eaT_sb"); ef_ps = sem("ef_ps"); ef_sb = sem("ef_sb")
        kT_ps = sem("kT_ps"); kT_sb = sem("kT_sb"); same_set = sem("same_set"); count_set = sem("count_set")
        dest_a = sem("dest_a"); dest_b = sem("dest_b"); dest_set = sem("dest_set")
        st_set = sem("st_set"); mv_set = sem("mv_set"); sd_set = sem("sd_set"); rs_set = sem("rs_set"); nm_set = sem("nm_set")
        h_set = sem("h_set"); msg_set = sem("msg_set"); tot_ps = sem("tot_ps"); pay_set = sem("pay_set")

        with ExitStack() as scope:
            def ring(name, shape, dt=f32):
                return [sb(f"{name}{n}", shape, dt, scope) for n in range(R)]
            xs = ring("xs", [P, J, D]); sgi = ring("sgi", [P, J], i32); ea = ring("ea", [P, J * DE])
            eaT = ring("eaT", [J * DE, P]); ef = ring("ef", [P, J, D]); kT = ring("kT", [P, GE])
            same = ring("same", [P, J, GE]); junk = sb("junk", [P, J, GE], f32, scope)
            own = ring("own", [P, J]); count = ring("count", [P, J]); gap = ring("gap", [P, J]); hop = ring("hop", [P, J])
            dest = ring("dest", [P, J], i32)
            st = ring("st", [P, J, 6]); mv = ring("mv", [P, J, 2]); sd = ring("sd", [P, J])
            rs = ring("rs", [P, J]); nm = ring("nm", [P, J]); hs = ring("hs", [P, J, D])
            msg = ring("msg", [P, J, D]); pay = ring("pay", [P, J, D])
            eaT_p, ef_p = psum[0][:, 0:P], psum[0][:, BANK:2 * BANK]
            kT_p, tot_p = psum[1][:, 0:BANK], psum[2][:, 0:BANK]

            with nc.Block() as block:
                @block.sync
                def _(sp):
                    def load_attr(i, u):
                        k = R * i + u
                        n = EREST if isinstance(k, int) and k == EFULL else P
                        if isinstance(k, int) and k > EFULL:
                            return
                        wait(sp, eaT_ps, k - R + 1)
                        sp.dma_start(ea[u][0:n, :], edge_rows(k)).then_inc(ea_in[u], 16)
                    steps(sp, NG, R, load_attr, 2)

                @block.gpsimd
                def _(pool):
                    def gather(i, u):
                        k = R * i + u
                        wait(pool, h_set, k - R + 1)
                        pool.sem_inc(go2, 1)
                        pool.tensor_copy(sgi[u][:, :], src_i[:, bass.ds(k, 1), :].rearrange("p a j -> p (a j)")).then_inc(gi_set, 1)
                        wait(pool, gi_set, k + 1)
                        pool.sem_inc(go2, 1)
                        for j in range(J):
                            pool.indirect_dma_start(
                                out=xs[u][:, j, :], out_offset=None, in_=x[:, :],
                                in_offset=bass.IndirectOffsetOnAxis(ap=sgi[u][:, j:j + 1], axis=0)).then_inc(xs_got[u], 16)

                    def gather_then_add(i, u):
                        k = R * i + u
                        if not (isinstance(k, int) and k + 2 >= NG):
                            gather(i + (u + 2) // R, (u + 2) % R)
                        wait(pool, pay_set, k + 1)
                        wait(pool, dest_set, k + 1)
                        wait(pool, sent[(u - 1) % R], 16 * J * (i + (u + 2) // R))
                        pool.sem_inc(go2, 1)
                        for j in range(J):
                            pool.indirect_dma_start(
                                out=agg[:, :], out_offset=bass.IndirectOffsetOnAxis(ap=dest[u][:, j:j + 1], axis=0),
                                in_=pay[u][:, j, :], in_offset=None, compute_op=ALU.add).then_inc(sent[u], 16)
                    gather(0, 0)
                    gather(0, 1)
                    steps(pool, NG, R, gather_then_add, 2)
                    for u in range(R):
                        pool.wait_ge(sent[u], 16 * J * ((NG - u + R - 1) // R))

                @block.vector
                def _(dve):
                    def own_keys(i, u):
                        k = R * i + u
                        wait(dve, kT_ps, k - R + 1)
                        dve.tensor_copy(own[u][:, :], dst_k[:, bass.ds(k, 1), :].rearrange("p a j -> p (a j)")).then_inc(own_set, 1)

                    def places(i, u):
                        k = R * i + u
                        wait(dve, own_set, k + 1)
                        wait(dve, kT_sb, k + 1)
                        wait(dve, tot_ps, k - R + 1)
                        for j in range(J):
                            dve.tensor_scalar(same[u][:, j, :], kT[u][:, :], own[u][:, j:j + 1], None,
                                              ALU.is_equal).then_inc(same_set, 1)
                        for j in range(J):
                            wait(dve, same_set, J * k + j + 1)
                            dve.tensor_tensor_reduce(out=junk[:, j, 0:(j + 1) * P], in0=same[u][:, j, 0:(j + 1) * P],
                                                     in1=earlier[:, GE - (j + 1) * P:GE], scale=1.0, scalar=0.0,
                                                     op0=ALU.mult, op1=ALU.add,
                                                     accum_out=count[u][:, j:j + 1]).then_inc(count_set, 1)
                        wait(dve, pay_set, k - R + 1)
                        wait(dve, sent[u], 16 * J * i)
                        dve.tensor_tensor(gap[u][:, :], trash[:, :], own[u][:, :],
                                          ALU.subtract).then_inc(dest_a, 1)
                        wait(dve, dest_a, k + 1)
                        wait(dve, count_set, J * (k + 1))
                        dve.scalar_tensor_tensor(out=hop[u][:, :], in0=count[u][:, :], scalar=0.0, in1=gap[u][:, :],
                                                 op0=ALU.is_gt, op1=ALU.mult).then_inc(dest_b, 1)
                        wait(dve, dest_b, k + 1)
                        dve.tensor_tensor(dest[u][:, :], hop[u][:, :], own[u][:, :],
                                          ALU.add).then_inc(dest_set, 1)

                    def norms(i, u):
                        k = R * i + u
                        wait(dve, xs_got[u], 16 * J * (i + 1))
                        for j in range(J):
                            dve.bn_stats(st[u][:, j, :], xs[u][:, j, :]).then_inc(st_set, 1)
                        wait(dve, st_set, J * (k + 1))
                        dve.sem_inc(dve_go, 1)
                        for j in range(J):
                            dve.bn_aggr(mv[u][:, j, :], st[u][:, j, :]).then_inc(mv_set, 1)
                        wait(dve, sd_set, k + 1)
                        dve.reciprocal(rs[u][:, :], sd[u][:, :]).then_inc(rs_set, 1)
                        wait(dve, rs_set, k + 1)
                        dve.scalar_tensor_tensor(out=nm[u][:, :], in0=mv[u][:, :, 0], scalar=-1.0, in1=rs[u][:, :],
                                                 op0=ALU.mult, op1=ALU.mult).then_inc(nm_set, 1)
                        wait(dve, h_set, k + 1)
                        wait(dve, ef_sb, k + 1)
                        dve.tensor_tensor(msg[u][:, :, :], hs[u][:, :, :], ef[u][:, :, :], ALU.add).then_inc(msg_set, 1)

                    def step(i, u):
                        k = R * i + u
                        if not (isinstance(k, int) and k + 2 >= NG):
                            own_keys(i + (u + 2) // R, (u + 2) % R)
                        if not (isinstance(k, int) and k + 1 >= NG):
                            places(i + (u + 1) // R, (u + 1) % R)
                        norms(i, u)
                    own_keys(0, 0)
                    own_keys(0, 1)
                    places(0, 0)
                    steps(dve, NG, R, step, 2)

                @block.scalar
                def _(act):
                    def keys_and_features(i, u):
                        k = R * i + u
                        wait(act, kT_ps, k + 1)
                        wait(act, count_set, J * (k - R + 1))
                        act.activation(kT[u][:, :], kT_p, ACT.Copy).then_inc(kT_sb, 1)
                        wait(act, eaT_ps, k + 1)
                        wait(act, ef_ps, k - R + 1)
                        act.activation(eaT[u][:, :], eaT_p, ACT.Copy).then_inc(eaT_sb, 1)
                        wait(act, ef_ps, k + 1)
                        wait(act, msg_set, k - R + 1)
                        act.activation(ef[u][:, :, :].rearrange("p j d -> p (j d)"), ef_p, ACT.Relu).then_inc(ef_sb, 1)

                    def norms(i, u):
                        k = R * i + u
                        wait(act, mv_set, J * (k + 1))
                        act.activation(sd[u][:, :], mv[u][:, :, 1], ACT.Sqrt, bias=lneps[:, 0:1]).then_inc(sd_set, 1)
                        wait(act, nm_set, k + 1)
                        wait(act, msg_set, k - R + 1)
                        for j in range(J):
                            a = act.activation(hs[u][:, j, :], xs[u][:, j, :], ACT.Relu, bias=nm[u][:, j:j + 1],
                                               scale=rs[u][:, j:j + 1])
                        a.then_inc(h_set, 1)
                        wait(act, tot_ps, k + 1)
                        wait(act, sent[u], 16 * J * i)
                        act.activation(pay[u][:, :, :].rearrange("p j d -> p (j d)"), tot_p, ACT.Copy).then_inc(pay_set, 1)

                    def step(i, u):
                        if not (isinstance(i, int) and R * i + u + 1 >= NG):
                            keys_and_features(i + (u + 1) // R, (u + 1) % R)
                        norms(i, u)
                    keys_and_features(0, 0)
                    steps(act, NG, R, step, 1)

                @block.tensor
                def _(pe):
                    def keys_and_features(i, u):
                        k = R * i + u
                        wait(pe, own_set, k + 1)
                        wait(pe, kT_sb, k)
                        for j in range(J):
                            m = nc.tensor.transpose(kT_p[:, j * P:(j + 1) * P], own[u][:, j:j + 1].broadcast_to((P, P)), ident[:, :])
                        m.then_inc(kT_ps, 1)
                        if not (isinstance(k, int) and k > EFULL):
                            wait(pe, ea_in[u], 16 * (i + 1))
                        wait(pe, eaT_sb, k)
                        nc.tensor.transpose(eaT_p, ea[u][:, :], ident[:, :]).then_inc(eaT_ps, 1)
                        wait(pe, eaT_sb, k + 1)
                        wait(pe, ef_sb, k)
                        nc.tensor.matmul(ef_p, eaT[u][:, :], WeB[:, :], start=True, stop=False)
                        nc.tensor.matmul(ef_p, ones[0:1, :], beB[0:1, :], start=False, stop=True).then_inc(ef_ps, 1)

                    def sums(i, u):
                        k = R * i + u
                        wait(pe, msg_set, k + 1)
                        wait(pe, same_set, J * (k + 1))
                        wait(pe, pay_set, k)
                        for o in range(J):
                            for j in range(J):
                                m = nc.tensor.matmul(tot_p[:, o * D:(o + 1) * D], same[u][:, j, o * P:(o + 1) * P],
                                                     msg[u][:, j, :], start=(j == 0), stop=(j == J - 1))
                        m.then_inc(tot_ps, 1)

                    def step(i, u):
                        if not (isinstance(i, int) and R * i + u + 1 >= NG):
                            keys_and_features(i + (u + 1) // R, (u + 1) % R)
                        sums(i, u)
                    keys_and_features(0, 0)
                    steps(pe, NG, R, step, 1)

        B = 4
        NT = NB + NE

        def blocks(eng, step):
            for u in range(B):
                step(0, u, False)
            with eng.Fori(1, NB // B) as i:
                for u in range(B):
                    step(i, u, False)
            turn = -(-(NB + 1) // B)
            for k in range(NB // B * B, turn * B):
                step(k // B, k % B, k >= NB)
            stop = (NT - 1) // B
            with eng.Fori(turn, stop) as i:
                for u in range(B):
                    step(i, u, True)
            for k in range(stop * B, NT):
                step(k // B, k % B, True)

        def at(i, u, by, of_edges):
            k = B * i + u + by
            if isinstance(i, int):
                return k // B, k % B, k >= NB
            return i + (u + by) // B, (u + by) % B, of_edges

        def exists(k):
            return not isinstance(k, int) or 0 <= k < NT

        def uses(u):
            return (NT - u + B - 1) // B

        def tail(k):
            return isinstance(k, int) and k == NB - 1

        def stat_slices(k, y):
            if tail(k):
                return [(2 * (NB - 1) + c, y[:, c * P + SEEN:(c + 1) * P]) for c in range(C)]
            return [(2 * k + h, y[:, h * BANK:(h + 1) * BANK]) for h in range(2)]

        def edge_block(table, k):
            return table[bass.ds(2 * (k - NB), 2), :, :].rearrange("g p f -> p g f")

        def half(t):
            return t.rearrange("p (g c) d -> p g (c d)", g=2)

        def batch_norm(dve, n, mvt, tmp):
            b, g, beta = (cols[:, 3 * n + m:3 * n + m + 1] for m in range(3))
            c0 = 6 * n

            def link(ins, m):
                ins.then_inc(bn_chain, 1)
                dve.wait_ge(bn_chain, c0 + m)
            link(dve.bn_aggr(mvt[:, 0:2], stat[:, :, :].rearrange("p s f -> p (s f)")), 1)
            dve.wait_ge(bn_root, n + 1)
            link(dve.reciprocal(tmp[:, 1:2], tmp[:, 0:1]), 2)
            link(dve.tensor_tensor(bn_s[:, n:n + 1], g, tmp[:, 1:2], ALU.mult), 3)
            link(dve.tensor_tensor(tmp[:, 2:3], mvt[:, 0:1], b, ALU.add), 4)
            link(dve.tensor_tensor(tmp[:, 3:4], b, tmp[:, 2:3], ALU.subtract), 5)
            link(dve.scalar_tensor_tensor(out=bn_t[:, n:n + 1], in0=tmp[:, 3:4], scalar=bn_s[:, n:n + 1], in1=beta,
                                          op0=ALU.mult, op1=ALU.add), 6)

        bn_chain = sem("bn_chain"); bn_root = sem("bn_root")
        yc = sb("yc", [P, NE, BN])

        p1_in = [sem(f"p1_in{n}") for n in range(B)]; p1_ain = [sem(f"p1_ain{n}") for n in range(B)]
        p1_st = sem("p1_st"); p1_mv = sem("p1_mv"); p1_sd = sem("p1_sd"); p1_rs = sem("p1_rs"); p1_nm = sem("p1_nm")
        p1_h = sem("p1_h"); p1_h1 = sem("p1_h1"); p1_tp = sem("p1_tp"); p1_hT = sem("p1_hT"); p1_y = sem("p1_y")
        p1_bn = sem("p1_bn"); p1_ev = sem("p1_ev"); p1_out = [sem(f"p1_out{n}") for n in range(2)]
        ad_idx = sem("ad_idx"); ad_got = sem("ad_got"); ad_kept = sem("ad_kept"); go3 = sem("go3")

        with ExitStack() as scope:
            def ring(name, shape, n=B):
                return [sb(f"{name}_{m}", shape, f32, scope) for m in range(n)]
            xb = ring("xb", [P, C, D], n=2); ab = ring("ab", [P, C, D], n=2); h1 = ring("h1", [P, C, D], n=2)
            hT = ring("hT", [P, BN], n=2); yb = ring("yb", [P, BN], n=2)
            st = ring("pst", [P, C, 6]); mv = ring("pmv", [P, C, 2]); sd = ring("psd", [P, C]); rs = ring("prs", [P, C]); nm = ring("pnm", [P, C])
            adb = sb("adb", [P, J, D], f32, scope); agi = sb("agi", [P, J], i32, scope)
            mvt = sb("mvt", [P, 2], f32, scope); tmp = sb("tmp", [P, 4], f32, scope)

            with nc.Block() as block:
                @block.sync
                def _(sp):
                    def load(i, u, of_edges):
                        k = B * i + u
                        wait(sp, p1_h, k - 1)
                        if of_edges:
                            if isinstance(k, int) and k == NB:
                                sp.wait_ge(ad_kept, 16 * NG)
                            sp.dma_start(half(xb[u % 2][:, :, :]), edge_block(xd_c, k)).then_inc(p1_in[u], 16)
                        else:
                            sp.dma_start(xb[u % 2][:, :, :].rearrange("p c d -> p (c d)"), node_rows(x, k)).then_inc(p1_in[u], 16)
                        wait(sp, p1_h1, k - 1)
                        if of_edges:
                            sp.dma_start(half(ab[u % 2][:, :, :]), edge_block(ad_c, k)).then_inc(p1_ain[u], 16)
                        else:
                            sp.dma_start(ab[u % 2][:, :, :].rearrange("p c d -> p (c d)"), node_rows(agg, k)).then_inc(p1_ain[u], 16)
                    blocks(sp, load)

                @block.gpsimd
                def _(pool):
                    def gather_ad(k):
                        wait(pool, ad_kept, 16 * k)
                        pool.sem_inc(go3, 1)
                        pool.tensor_copy(agi[:, :], dst_i[:, bass.ds(k, 1), :].rearrange("p a j -> p (a j)")).then_inc(ad_idx, 1)
                        wait(pool, ad_idx, k + 1)
                        pool.sem_inc(go3, 1)
                        for j in range(J):
                            pool.indirect_dma_start(
                                out=adb[:, j, :], out_offset=None, in_=agg[:, :],
                                in_offset=bass.IndirectOffsetOnAxis(ap=agi[:, j:j + 1], axis=0)).then_inc(ad_got, 16)
                        wait(pool, ad_got, 16 * J * (k + 1))
                        pool.sem_inc(go3, 1)
                        pool.dma_start(ad_c[bass.ds(k, 1), :, :].rearrange("a p f -> p (a f)"),
                                       adb[:, :, :].rearrange("p j d -> p (j d)")).then_inc(ad_kept, 16)
                    gather_ad(0)
                    with pool.Fori(1, NG) as k:
                        gather_ad(k)
                    pool.wait_ge(ad_kept, 16 * NG)

                @block.vector
                def _(dve):
                    def norms(i, u, of_edges):
                        k = B * i + u
                        wait(dve, p1_in[u], 16 * (i + 1))
                        for c in range(C):
                            dve.bn_stats(st[u][:, c, :], xb[u % 2][:, c, :]).then_inc(p1_st, 1)
                        wait(dve, p1_st, C * (k + 1))
                        dve.sem_inc(dve_go, 1)
                        for c in range(C):
                            m = dve.bn_aggr(mv[u][:, c, :], st[u][:, c, :])
                        m.then_inc(p1_mv, 1)
                        wait(dve, p1_sd, k + 1)
                        dve.reciprocal(rs[u][:, :], sd[u][:, :]).then_inc(p1_rs, 1)
                        wait(dve, p1_rs, k + 1)
                        dve.scalar_tensor_tensor(out=nm[u][:, :], in0=mv[u][:, :, 0], scalar=-1.0, in1=rs[u][:, :],
                                                 op0=ALU.mult, op1=ALU.mult).then_inc(p1_nm, 1)

                    def finish(i, u, of_edges):
                        k = B * i + u
                        wait(dve, p1_h, k + 1)
                        wait(dve, p1_ain[u], 16 * (i + 1))
                        flat = h1[u % 2][:, :, :].rearrange("p c d -> p (c d)")
                        dve.scalar_tensor_tensor(out=flat, in0=flat, scalar=epst[:, 0:1],
                                                 in1=ab[u % 2][:, :, :].rearrange("p c d -> p (c d)"),
                                                 op0=ALU.mult, op1=ALU.add).then_inc(p1_h1, 1)

                    def stats(i, u, of_edges):
                        k = B * i + u
                        if of_edges:
                            return
                        wait(dve, p1_ev, k + 1)
                        for n, part in stat_slices(k, yb[u % 2]):
                            m = dve.bn_stats(stat[:, n, :] if isinstance(n, int) else
                                             stat[:, bass.ds(n, 1), :].rearrange("p a f -> p (a f)"), part)
                        m.then_inc(p1_bn, 1)

                    def step(i, u, of_edges):
                        k = B * i + u
                        if exists(k + 1):
                            norms(*at(i, u, 1, of_edges))
                        finish(i, u, of_edges)
                        if exists(k - 1):
                            stats(*at(i, u, -1, of_edges))
                    norms(0, 0, False)
                    blocks(dve, step)
                    dve.wait_ge(p1_bn, NB)
                    batch_norm(dve, 0, mvt, tmp)

                @block.scalar
                def _(act):
                    def norms(i, u, of_edges):
                        k = B * i + u
                        wait(act, p1_mv, k + 1)
                        act.activation(sd[u][:, :], mv[u][:, :, 1], ACT.Sqrt, bias=lneps[:, 0:1]).then_inc(p1_sd, 1)
                        wait(act, p1_nm, k + 1)
                        wait(act, p1_tp, k - 1)
                        for c in range(C):
                            a = act.activation(h1[u % 2][:, c, :], xb[u % 2][:, c, :], ACT.Relu, bias=nm[u][:, c:c + 1],
                                               scale=rs[u][:, c:c + 1])
                        a.then_inc(p1_h, 1)

                    def finish(i, u, of_edges):
                        k = B * i + u
                        wait(act, p1_tp, k + 1)
                        wait(act, p1_y, k - 1)
                        act.activation(hT[u % 2][:, :], psum[u % 2][:, :], ACT.Copy).then_inc(p1_hT, 1)

                    def keep(i, u, of_edges):
                        k = B * i + u
                        wait(act, p1_y, k + 1)
                        if of_edges:
                            act.activation(yc[:, bass.ds(k - NB, 1), :].rearrange("p a f -> p (a f)"),
                                           psum[2 + u % 2][:, :], ACT.Copy).then_inc(p1_ev, 1)
                            return
                        wait(act, p1_out[u % 2], 16 * (2 * i + u // 2))
                        wait(act, p1_bn, k - 1)
                        act.activation(yb[u % 2][:, :], psum[2 + u % 2][:, :], ACT.Copy).then_inc(p1_ev, 1)
                        wait(act, p1_ev, k + 1)
                        act.dma_start(y1_s[bass.ds(k, 1), :, :].rearrange("a p f -> p (a f)"), yb[u % 2][:, :]).then_inc(p1_out[u % 2], 16)

                    def step(i, u, of_edges):
                        k = B * i + u
                        if exists(k + 1):
                            norms(*at(i, u, 1, of_edges))
                        finish(i, u, of_edges)
                        if exists(k - 1):
                            keep(*at(i, u, -1, of_edges))
                    norms(0, 0, False)
                    blocks(act, step)
                    keep(*at((NT - 1) // B, (NT - 1) % B, 0, True))
                    act.wait_ge(bn_chain, 1)
                    act.activation(tmp[:, 0:1], mvt[:, 1:2], ACT.Sqrt, bias=lneps[:, 0:1]).then_inc(bn_root, 1)
                    for u in range(2):
                        act.wait_ge(p1_out[u], 16 * NB // 2)

                @block.tensor
                def _(pe):
                    def step(i, u, of_edges):
                        k = B * i + u
                        wait(pe, p1_h1, k + 1)
                        wait(pe, p1_hT, k - 1)
                        for c in range(C):
                            m = nc.tensor.transpose(psum[u % 2][:, c * P:(c + 1) * P], h1[u % 2][:, c, :], ident[:, :])
                        m.then_inc(p1_tp, 1)
                        wait(pe, p1_hT, k + 1)
                        wait(pe, p1_ev, k - 1)
                        for h in range(2):
                            m = nc.tensor.matmul(psum[2 + u % 2][:, h * BANK:(h + 1) * BANK], w1[:, :],
                                                 hT[u % 2][:, h * BANK:(h + 1) * BANK], start=True, stop=True)
                        m.then_inc(p1_y, 1)
                    blocks(pe, step)

        p2_in = [sem(f"p2_in{n}") for n in range(B)]; p2_z = sem("p2_z"); p2_y = sem("p2_y"); p2_bn = sem("p2_bn")
        p2_ev = sem("p2_ev"); p2_out = [sem(f"p2_out{n}") for n in range(2)]

        with ExitStack() as scope:
            def ring(name, shape, n=B):
                return [sb(f"{name}_{m}", shape, f32, scope) for m in range(n)]
            ub = ring("ub", [P, BN]); z1 = ring("z1", [P, BN], n=2); vb = ring("vb", [P, BN], n=2)
            mvt = sb("mvt2", [P, 2], f32, scope); tmp = sb("tmp2", [P, 4], f32, scope)

            with nc.Block() as block:
                @block.sync
                def _(sp):
                    def load(i, u, of_edges):
                        k = B * i + u
                        if of_edges:
                            return
                        wait(sp, p2_z, k - B + 1)
                        sp.dma_start(ub[u][:, :], y1_s[bass.ds(k, 1), :, :].rearrange("a p f -> p (a f)")).then_inc(p2_in[u], 16)
                    steps(sp, NB, B, lambda i, u: load(i, u, False), 2)

                @block.scalar
                def _(act):
                    def step(i, u, of_edges):
                        k = B * i + u
                        wait(act, p2_y, k - 1)
                        if of_edges:
                            y = yc[:, bass.ds(k - NB, 1), :].rearrange("p a f -> p (a f)")
                        else:
                            wait(act, p2_in[u], 16 * (i + 1))
                            y = ub[u][:, :]
                        act.activation(z1[u % 2][:, :], y, ACT.Relu, bias=bn_t[:, 0:1], scale=bn_s[:, 0:1]).then_inc(p2_z, 1)
                    blocks(act, step)
                    act.wait_ge(bn_chain, 7)
                    act.activation(tmp[:, 0:1], mvt[:, 1:2], ACT.Sqrt, bias=lneps[:, 0:1]).then_inc(bn_root, 1)

                @block.gpsimd
                def _(pool):
                    def keep(i, u):
                        k = B * i + u
                        wait(pool, p2_ev, k + 1)
                        pool.sem_inc(go3, 1)
                        pool.dma_start(y2_s[bass.ds(k, 1), :, :].rearrange("a p f -> p (a f)"), vb[u % 2][:, :]).then_inc(p2_out[u % 2], 16)
                    steps(pool, NB, B, keep, 2)
                    for u in range(2):
                        pool.wait_ge(p2_out[u], 16 * NB // 2)

                @block.vector
                def _(dve):
                    def step(i, u, of_edges):
                        k = B * i + u
                        wait(dve, p2_y, k + 1)
                        if of_edges:
                            dve.tensor_copy(yc[:, bass.ds(k - NB, 1), :].rearrange("p a f -> p (a f)"), psum[u][:, :]).then_inc(p2_ev, 1)
                            return
                        for n, part in stat_slices(k, psum[u]):
                            m = dve.bn_stats(stat[:, n, :] if isinstance(n, int) else
                                             stat[:, bass.ds(n, 1), :].rearrange("p a f -> p (a f)"), part)
                        m.then_inc(p2_bn, 1)
                        wait(dve, p2_out[u % 2], 16 * (2 * i + u // 2))
                        dve.tensor_copy(vb[u % 2][:, :], psum[u][:, :]).then_inc(p2_ev, 1)
                    blocks(dve, step)
                    dve.wait_ge(p2_bn, NB)
                    batch_norm(dve, 1, mvt, tmp)

                @block.tensor
                def _(pe):
                    def step(i, u, of_edges):
                        k = B * i + u
                        wait(pe, p2_z, k + 1)
                        wait(pe, p2_ev, k - 3)
                        for h in range(2):
                            m = nc.tensor.matmul(psum[u][:, h * BANK:(h + 1) * BANK], w2[:, :],
                                                 z1[u % 2][:, h * BANK:(h + 1) * BANK], start=True, stop=True)
                        m.then_inc(p2_y, 1)
                    blocks(pe, step)

        p3_in = [sem(f"p3_in{n}") for n in range(B)]; p3_xin = [sem(f"p3_xin{n}") for n in range(B)]
        p3_z = sem("p3_z"); p3_zb = sem("p3_zb"); p3_tp = sem("p3_tp"); p3_x2 = sem("p3_x2"); p3_out = [sem(f"p3_out{n}") for n in range(2)]
        d_idx = sem("d_idx"); d_got = sem("d_got"); d_kept = sem("d_kept"); d_prod = sem("d_prod")
        norm = sb("norm", [P, NG, J])
        norm2 = sb("norm2", [P, NG, J])

        with ExitStack() as scope:
            def ring(name, shape, n=2):
                return [sb(f"{name}_{m}", shape, f32, scope) for m in range(n)]
            yb = ring("yb3", [P, BN]); xb = ring("xb3", [P, C, D]); zb = ring("zb3", [P, BN]); ob = ring("ob3", [P, C, D])
            gi = [sb(f"gi{n}", [P, J], i32, scope) for n in range(2)]
            gv = ring("gv", [P, J])

            with nc.Block() as block:
                @block.sync
                def _(sp):
                    def load(i, u, of_edges):
                        k = B * i + u
                        if not of_edges:
                            wait(sp, p3_z, k - 1)
                            sp.dma_start(yb[u % 2][:, :], y2_s[bass.ds(k, 1), :, :].rearrange("a p f -> p (a f)")).then_inc(p3_in[u], 16)
                        wait(sp, p3_x2, k - 1)
                        if of_edges:
                            sp.dma_start(half(xb[u % 2][:, :, :]), edge_block(xd_c, k)).then_inc(p3_xin[u], 16)
                        else:
                            sp.dma_start(xb[u % 2][:, :, :].rearrange("p c d -> p (c d)"), node_rows(x, k)).then_inc(p3_xin[u], 16)
                    blocks(sp, load)

                @block.scalar
                def _(act):
                    def step(i, u, of_edges):
                        k = B * i + u
                        if of_edges:
                            y = yc[:, bass.ds(k - NB, 1), :].rearrange("p a f -> p (a f)")
                        else:
                            wait(act, p3_in[u], 16 * (i + 1))
                            y = yb[u % 2][:, :]
                        wait(act, p3_tp, k - 1)
                        act.activation(zb[u % 2][:, :], y, ACT.Relu, bias=bn_t[:, 1:2], scale=bn_s[:, 1:2]).then_inc(p3_z, 1)
                        if exists(k - 1):
                            keep(*at(i, u, -1, of_edges))

                    def keep(i, u, of_edges):
                        k = B * i + u
                        wait(act, p3_x2, k + 1)
                        o = ob[u % 2][:, :, :]
                        if of_edges:
                            act.dma_start(edge_block(x2_c, k), half(o)).then_inc(p3_out[u % 2], 16)
                        else:
                            lo = SEEN if tail(k) else 0
                            act.dma_start(node_rows(out, k, lo), o[lo:P, :, :].rearrange("p c d -> p (c d)")).then_inc(p3_out[u % 2], 16)
                    blocks(act, step)
                    keep(*at((NT - 1) // B, (NT - 1) % B, 0, True))
                    for u in range(2):
                        act.wait_ge(p3_out[u], 16 * ((NT - u + 1) // 2))

                @block.tensor
                def _(pe):
                    def step(i, u, of_edges):
                        k = B * i + u
                        wait(pe, p3_zb, k + 1)
                        wait(pe, p3_x2, k - 3)
                        for c in range(C):
                            m = nc.tensor.transpose(psum[u][:, c * P:(c + 1) * P], zb[u % 2][:, c * P:(c + 1) * P], ident[:, :])
                        m.then_inc(p3_tp, 1)
                    blocks(pe, step)

                @block.vector
                def _(dve):
                    def bias(i, u, of_edges):
                        k = B * i + u
                        wait(dve, p3_z, k + 1)
                        if of_edges:
                            dve.sem_inc(p3_zb, 1)
                            return
                        dve.tensor_scalar(zb[u % 2][:, :], zb[u % 2][:, :], cols[:, 6:7], None, ALU.add).then_inc(p3_zb, 1)

                    def add_x(i, u, of_edges):
                        k = B * i + u
                        wait(dve, p3_tp, k + 1)
                        wait(dve, p3_xin[u], 16 * (i + 1))
                        wait(dve, p3_out[u % 2], 16 * (2 * i + u // 2))
                        dve.tensor_tensor(ob[u % 2][:, :, :].rearrange("p c d -> p (c d)"), psum[u][:, :],
                                          xb[u % 2][:, :, :].rearrange("p c d -> p (c d)"), ALU.add).then_inc(p3_x2, 1)

                    def step(i, u, of_edges):
                        if exists(B * i + u + 1):
                            bias(*at(i, u, 1, of_edges))
                        add_x(i, u, of_edges)
                    bias(0, 0, False)
                    blocks(dve, step)
                    dve.wait_ge(d_kept, 2 * NG)
                    dve.tensor_tensor(norm[:, :, :], norm[:, :, :], norm2[:, :, :], ALU.mult).then_inc(d_prod, 1)

                @block.gpsimd
                def _(pool):
                    def ends(k):
                        for n, table in enumerate((src_i, dst_i)):
                            wait(pool, d_got, 16 * J * (2 * k + n))
                            pool.sem_inc(go3, 1)
                            pool.tensor_copy(gi[n][:, :], table[:, bass.ds(k, 1), :].rearrange("p a j -> p (a j)")).then_inc(d_idx, 1)
                            wait(pool, d_idx, 2 * k + n + 1)
                            pool.sem_inc(go3, 1)
                            for j in range(J):
                                pool.indirect_dma_start(
                                    out=gv[n][:, j:j + 1], out_offset=None, in_=dis_tab[:, :],
                                    in_offset=bass.IndirectOffsetOnAxis(ap=gi[n][:, j:j + 1], axis=0)).then_inc(d_got, 16)
                        wait(pool, d_got, 16 * J * (2 * k + 2))
                        pool.sem_inc(go3, 1)
                        for n, t in enumerate((norm, norm2)):
                            pool.tensor_copy(t[:, bass.ds(k, 1), :].rearrange("p a j -> p (a j)"), gv[n][:, :]).then_inc(d_kept, 1)
                        wait(pool, d_kept, 2 * k + 2)
                        pool.sem_inc(go3, 1)
                    ends(0)
                    with pool.Fori(1, NG) as k:
                        ends(k)

        e_in = [sem(f"e_in{n}") for n in range(R)]; e_sent = [sem(f"e_sent{n}") for n in range(R)]; go5 = sem("go5"); e_own = sem("e_own")
        e_kps = sem("e_kps"); e_ksb = sem("e_ksb"); e_same = sem("e_same"); e_cnt = sem("e_cnt")
        e_da = sem("e_da"); e_db = sem("e_db"); e_dest = sem("e_dest")
        e_st = sem("e_st"); e_mv = sem("e_mv"); e_sd = sem("e_sd"); e_rs = sem("e_rs"); e_nm = sem("e_nm"); e_h = sem("e_h")
        e_tp = sem("e_tp"); e_hT = sem("e_hT"); e_w = sem("e_w"); e_msg = sem("e_msg"); e_tot = sem("e_tot"); e_pay = sem("e_pay")

        with ExitStack() as scope:
            def ring(name, shape, dt=f32):
                return [sb(f"{name}_e{n}", shape, dt, scope) for n in range(R)]
            xs = ring("xs", [P, J, D]); kT = ring("kT", [P, GE]); same = [yc[:, 2 * n:2 * n + 2, :].rearrange("p a (b e) -> p (a b) e", e=GE) for n in range(R)]
            junk = sb("junk_e", [P, J, GE], f32, scope)
            own = ring("own", [P, J]); count = ring("count", [P, J]); gap = ring("gap", [P, J]); hop = ring("hop", [P, J]); dest = ring("dest", [P, J], i32)
            st = ring("st", [P, J, 6]); mv = ring("mv", [P, J, 2]); sd = ring("sd", [P, J]); rs = ring("rs", [P, J]); nm = ring("nm", [P, J])
            hs = ring("hs", [P, J, D]); hT = ring("hT", [P, GE]); msg = ring("msg", [P, J, D]); pay = ring("pay", [P, J, D])
            kT_p, hT_p, w_p, tot_p = psum[0][:, 0:BANK], psum[1][:, 0:BANK], psum[2][:, 0:BANK], psum[3][:, 0:BANK]

            with nc.Block() as block:
                @block.sync
                def _(sp):
                    def load(i, u):
                        k = R * i + u
                        wait(sp, e_h, k - R + 1)
                        sp.dma_start(xs[u][:, :, :].rearrange("p j d -> p (j d)"),
                                     x2_c[bass.ds(k, 1), :, :].rearrange("a p f -> p (a f)")).then_inc(e_in[u], 16)
                    steps(sp, NG, R, load, 1)

                @block.gpsimd
                def _(pool):
                    def add(i, u):
                        k = R * i + u
                        wait(pool, e_pay, k + 1)
                        wait(pool, e_dest, k + 1)
                        wait(pool, e_sent[(u - 1) % R], 16 * J * (i + (u + 2) // R))
                        pool.sem_inc(go5, 1)
                        for j in range(J):
                            pool.indirect_dma_start(
                                out=out[:, :], out_offset=bass.IndirectOffsetOnAxis(ap=dest[u][:, j:j + 1], axis=0),
                                in_=pay[u][:, j, :], in_offset=None, compute_op=ALU.add).then_inc(e_sent[u], 16)
                    steps(pool, NG, R, add, 1)
                    for u in range(R):
                        pool.wait_ge(e_sent[u], 16 * J * ((NG - u + R - 1) // R))

                @block.vector
                def _(dve):
                    def own_keys(i, u):
                        k = R * i + u
                        wait(dve, e_kps, k - R + 1)
                        dve.tensor_copy(own[u][:, :], src_k[:, bass.ds(k, 1), :].rearrange("p a j -> p (a j)")).then_inc(e_own, 1)

                    def places(i, u):
                        k = R * i + u
                        wait(dve, e_own, k + 1)
                        wait(dve, e_ksb, k + 1)
                        wait(dve, e_tot, k - R + 1)
                        for j in range(J):
                            dve.tensor_scalar(same[u][:, j, :], kT[u][:, :], own[u][:, j:j + 1], None,
                                              ALU.is_equal).then_inc(e_same, 1)
                        for j in range(J):
                            wait(dve, e_same, J * k + j + 1)
                            dve.tensor_tensor_reduce(out=junk[:, j, 0:(j + 1) * P], in0=same[u][:, j, 0:(j + 1) * P],
                                                     in1=earlier[:, GE - (j + 1) * P:GE], scale=1.0, scalar=0.0,
                                                     op0=ALU.mult, op1=ALU.add,
                                                     accum_out=count[u][:, j:j + 1]).then_inc(e_cnt, 1)
                        wait(dve, e_sent[u], 16 * J * i)
                        dve.tensor_tensor(gap[u][:, :], trash[:, :], own[u][:, :], ALU.subtract).then_inc(e_da, 1)
                        wait(dve, e_da, k + 1)
                        wait(dve, e_cnt, J * (k + 1))
                        dve.scalar_tensor_tensor(out=hop[u][:, :], in0=count[u][:, :], scalar=0.0, in1=gap[u][:, :],
                                                 op0=ALU.is_gt, op1=ALU.mult).then_inc(e_db, 1)
                        wait(dve, e_db, k + 1)
                        dve.tensor_tensor(dest[u][:, :], hop[u][:, :], own[u][:, :], ALU.add).then_inc(e_dest, 1)

                    def norms(i, u):
                        k = R * i + u
                        wait(dve, e_in[u], 16 * (i + 1))
                        for j in range(J):
                            dve.bn_stats(st[u][:, j, :], xs[u][:, j, :]).then_inc(e_st, 1)
                        wait(dve, e_st, J * (k + 1))
                        dve.sem_inc(dve_go, 1)
                        for j in range(J):
                            dve.bn_aggr(mv[u][:, j, :], st[u][:, j, :]).then_inc(e_mv, 1)
                        wait(dve, e_sd, k + 1)
                        dve.reciprocal(rs[u][:, :], sd[u][:, :]).then_inc(e_rs, 1)
                        wait(dve, e_rs, k + 1)
                        dve.scalar_tensor_tensor(out=nm[u][:, :], in0=mv[u][:, :, 0], scalar=-1.0, in1=rs[u][:, :],
                                                 op0=ALU.mult, op1=ALU.mult).then_inc(e_nm, 1)

                    def weigh(i, u):
                        k = R * i + u
                        wait(dve, e_w, k + 1)
                        wait(dve, e_tot, k - R + 1)
                        dve.tensor_tensor(msg[u][:, :, :], w_p.rearrange("p (j d) -> p j d", j=J),
                                          norm[:, bass.ds(k, 1), :].rearrange("p a j -> p j a").broadcast_to((P, J, D)),
                                          ALU.mult).then_inc(e_msg, 1)

                    def step(i, u):
                        k = R * i + u
                        if not (isinstance(k, int) and k + 2 >= NG):
                            own_keys(i + (u + 2) // R, (u + 2) % R)
                        if not (isinstance(k, int) and k + 1 >= NG):
                            norms(i + (u + 1) // R, (u + 1) % R)
                            places(i + (u + 1) // R, (u + 1) % R)
                        weigh(i, u)
                    own_keys(0, 0)
                    own_keys(0, 1)
                    norms(0, 0)
                    places(0, 0)
                    steps(dve, NG, R, step, 2)

                @block.scalar
                def _(act):
                    def ahead(i, u):
                        k = R * i + u
                        wait(act, e_kps, k + 1)
                        wait(act, e_cnt, J * (k - R + 1))
                        act.activation(kT[u][:, :], kT_p, ACT.Copy).then_inc(e_ksb, 1)
                        wait(act, e_mv, J * (k + 1))
                        act.activation(sd[u][:, :], mv[u][:, :, 1], ACT.Sqrt, bias=lneps[:, 0:1]).then_inc(e_sd, 1)
                        wait(act, e_nm, k + 1)
                        for j in range(J):
                            a = act.activation(hs[u][:, j, :], xs[u][:, j, :], ACT.Relu, bias=nm[u][:, j:j + 1],
                                               scale=rs[u][:, j:j + 1])
                        a.then_inc(e_h, 1)

                    def finish(i, u):
                        k = R * i + u
                        wait(act, e_tp, k + 1)
                        act.activation(hT[u][:, :], hT_p, ACT.Copy).then_inc(e_hT, 1)
                        wait(act, e_tot, k + 1)
                        wait(act, e_sent[u], 16 * J * i)
                        act.activation(pay[u][:, :, :].rearrange("p j d -> p (j d)"), tot_p, ACT.Copy).then_inc(e_pay, 1)

                    def step(i, u):
                        k = R * i + u
                        if not (isinstance(k, int) and k + 1 >= NG):
                            ahead(i + (u + 1) // R, (u + 1) % R)
                        finish(i, u)
                    ahead(0, 0)
                    steps(act, NG, R, step, 1)

                @block.tensor
                def _(pe):
                    def keys(i, u):
                        k = R * i + u
                        wait(pe, e_own, k + 1)
                        wait(pe, e_ksb, k)
                        for j in range(J):
                            m = nc.tensor.transpose(kT_p[:, j * P:(j + 1) * P], own[u][:, j:j + 1].broadcast_to((P, P)), ident[:, :])
                        m.then_inc(e_kps, 1)

                    def step(i, u):
                        k = R * i + u
                        if not (isinstance(k, int) and k + 1 >= NG):
                            keys(i + (u + 1) // R, (u + 1) % R)
                        wait(pe, e_h, k + 1)
                        for j in range(J):
                            m = nc.tensor.transpose(hT_p[:, j * P:(j + 1) * P], hs[u][:, j, :], ident[:, :])
                        m.then_inc(e_tp, 1)
                        wait(pe, e_hT, k + 1)
                        for j in range(J):
                            m = nc.tensor.matmul(w_p[:, j * D:(j + 1) * D], hT[u][:, j * P:(j + 1) * P], wlT[:, :], start=True, stop=True)
                        m.then_inc(e_w, 1)
                        wait(pe, e_msg, k + 1)
                        wait(pe, e_same, J * (k + 1))
                        wait(pe, e_pay, k)
                        for o in range(J):
                            for j in range(J):
                                m = nc.tensor.matmul(tot_p[:, o * D:(o + 1) * D], same[u][:, j, o * P:(o + 1) * P],
                                                     msg[u][:, j, :], start=(j == 0), stop=(j == J - 1))
                        m.then_inc(e_tot, 1)
                    keys(0, 0)
                    steps(pe, NG, R, step, 1)


_INS = ['x', 'src', 'dst', 'edge_attr_32', 'L0_gnn_epsilon', 'L0_gnn_We', 'L0_gnn_be', 'L0_gnn_W1', 'L0_gnn_b1',
        'L0_gnn_g1', 'L0_gnn_beta1', 'L0_gnn_W2', 'L0_gnn_b2', 'L0_gnn_g2', 'L0_gnn_beta2', 'L1_gnn_W', 'L1_gnn_b']
_ROWS = 786 * 128


def kernel(**inputs):
    import numpy as _np
    import concourse.bacc as _bacc
    from concourse import mybir as _mybir
    from concourse.bass_utils import run_bass_kernel_spmd as _run

    nc = _bacc.Bacc("TRN2", target_bir_lowering=False, num_devices=1)
    arrays, args = {}, []
    for name in _INS:
        a = _np.ascontiguousarray(inputs[name])
        arrays[f"in_{name}_dram"] = a
        args.append(nc.dram_tensor(f"in_{name}_dram", a.shape, _mybir.dt.from_np(a.dtype), kind="ExternalInput").ap())
    n, d = inputs["x"].shape
    args.append(nc.dram_tensor("out_0_dram", (_ROWS, d), _mybir.dt.float32, kind="ExternalOutput").ap())
    preln_gin_then_gcn(nc, *args)
    r = _run(nc, [arrays], core_ids=[0])
    return r.results[0]["out_0_dram"][:n]
```

```python
import concourse.bass as bass
from concourse import mybir
from contextlib import ExitStack


def preln_gin_then_gcn(nc, x, src, dst, edge_attr, epsilon, We, be, W1, b1, g1, beta1,
                       W2, b2, g2, beta2, Wl, bl, out):
    f32, bf16, i32 = mybir.dt.float32, mybir.dt.bfloat16, mybir.dt.int32
    ALU = mybir.AluOpType
    ACT = mybir.ActivationFunctionType

    N, D = x.shape
    E, DE = edge_attr.shape
    P = 128
    J = 4
    GE = P * J
    NG = 2 * -(-E // (2 * GE))
    NTILE = NG * J
    GFULL = E // GE
    TFULL = E // P
    TREST = E - TFULL * P
    C = 8
    BN = P * C
    NB = -(-N // BN)
    TAIL = N - BN
    SEEN = ((NB - 1) * BN - TAIL) // C
    BANK = 512
    PAD = N + GE
    ROWS = out.shape[0]
    EPS = 1e-5
    QB = 9
    QW = 1 << QB
    HALVES = -(-(PAD + 1) // (QW * P))
    B = 4
    NKEPT = NB // B
    R = 3
    assert NB == 2 * NG - 2 and NB % B == 2 and ROWS > PAD and (ROWS - N) % P == 0 and NG - 2 == GFULL and TREST > 0
    assert ((NB - 1) * BN - TAIL) % C == 0 and TFULL // J == GFULL

    table = nc.dram_tensor("gin_input", (ROWS, D), f32, kind="Internal").ap()
    dis_tab = nc.dram_tensor("inv_sqrt_degree", (HALVES * P * QW, 1), f32, kind="Internal").ap()
    y1_s = nc.dram_tensor("y1_feature_major", (NB, P, BN), f32, kind="Internal").ap()
    y2_s = nc.dram_tensor("y2_feature_major", (NB, P, BN), f32, kind="Internal").ap()

    def wait(eng, sem, value):
        if not (isinstance(value, int) and value <= 0):
            eng.wait_ge(sem, value)

    def steps(eng, n, ring, step, last):
        full = (n - last) // ring
        for u in range(ring):
            step(0, u)
        with eng.Fori(1, full) as i:
            for u in range(ring):
                step(i, u)
        for k in range(full * ring, n):
            step(k // ring, k % ring)

    def moved(i, u, by, ring):
        return i + (u + by) // ring, (u + by) % ring

    def inside(k, n):
        return not isinstance(k, int) or 0 <= k < n

    def tail(k):
        return isinstance(k, int) and k == NB - 1

    def node_rows(t, k, lo=0):
        base = TAIL if tail(k) else BN * k
        return t[bass.ds(base + lo * C, (P - lo) * C), :].rearrange("(p c) d -> p (c d)", c=C)

    def kept(t, k):
        return t[:, bass.ds(k, 1), :].rearrange("p a f -> p (a f)")

    def spilled(t, k):
        return t[bass.ds(k, 1), :, :].rearrange("a p f -> p (a f)")

    def flat(t):
        return t[:, :, :].rearrange("p a f -> p (a f)")

    ctx = ExitStack()
    with ctx:
        def sem(name):
            return ctx.enter_context(nc.semaphore(name))

        def sems(name, n):
            return [sem(f"{name}{m}") for m in range(n)]

        def sb(name, shape, dt=f32, scope=ctx):
            return scope.enter_context(nc.sbuf_tensor(name, shape, dt))

        def ring(name, n, shape, dt=f32, scope=ctx):
            return [sb(f"{name}{m}", shape, dt, scope) for m in range(n)]

        ident = sb("ident", [P, P])
        earlier = sb("earlier", [P, GE])
        trash = sb("trash", [P, J])
        src_i = sb("src_i", [P, NG, J], i32)
        dst_i = sb("dst_i", [P, NG, J], i32)
        src_k = sb("src_k", [P, NG, J])
        dst_k = sb("dst_k", [P, NG, J])
        norm = ring("norm", 2, [P, NG, J])
        w1 = sb("w1", [D, D])
        w2 = sb("w2", [D, D])
        wlT = sb("wlT", [D, D])
        blB = sb("blB", [P, D])
        gain = sb("gain", [P, C])
        sign = sb("sign", [P, 2])
        lneps = sb("lneps", [P, 1])
        cols = sb("cols", [P, 7])
        bn_s = sb("bn_s", [P, 2])
        bn_t = sb("bn_t", [P, 2])
        stat = sb("stat", [P, 2 * (NB - 1) + C, 6])
        big = sb("big", [P, max(NG * J * D, NKEPT * BN)])
        msgs = big[:, 0:NG * J * D].rearrange("p (g f) -> p g f", g=NG)
        ykept = big[:, 0:NKEPT * BN].rearrange("p (n f) -> p n f", n=NKEPT)
        psum = [ctx.enter_context(nc.psum_tensor(f"psum{n}", [P, 2 * BANK], f32)) for n in range(4)]
        pool_go = sem("pool_go"); dve_go = sem("dve_go")

        with ExitStack() as edge_scope:
            WeB = sb("WeB", [P, J * D], f32, edge_scope)
            beB = sb("beB", [1, J * D], f32, edge_scope)
            ones = sb("ones", [1, P], f32, edge_scope)

            params = sem("params"); indices = sem("indices"); cleared = sem("cleared"); const = sem("const")
            rows_f = sem("rows_f"); turned = sem("turned"); keys = sem("keys"); placed = sem("placed"); sized = sem("sized"); emptied = sem("emptied"); wl_turned = sem("wl_turned")
            N_PARAMS = 2 * J + 4 + 1 + 7
            TA = min(P, NTILE); TB = NTILE - TA
            with ExitStack() as scope:
                wl = sb("wl", [D, D], f32, scope)
                w1_raw = sb("w1_raw", [D, D], f32, scope)
                epst = sb("epst", [P, 1], f32, scope)
                eps1 = sb("eps1", [P, 2], f32, scope)
                unit = sb("unit", [P, C], f32, scope)
                trash_i = sb("trash_i", [P, J], i32, scope)
                zeros = sb("zeros", [P, (ROWS - N) // P * D], f32, scope)
                idx_i = [ring(f"idx_i{n}", 2, [P, P], i32, scope) for n in range(2)]
                idx_f = [ring(f"idx_f{n}", 2, [P, P], f32, scope) for n in range(2)]

                with nc.Block() as block:
                    @block.sync
                    def _(sp):
                        sp.wait_ge(cleared, 3)
                        for n, edges in enumerate((src, dst)):
                            a, b = idx_i[n]
                            sp.dma_start(a[:, :], edges[0:TA * P].rearrange("(t e) -> t e", e=P)).then_inc(indices, 16)
                            sp.dma_start(b[0:TFULL - TA, :], edges[TA * P:TFULL * P].rearrange("(t e) -> t e", e=P)).then_inc(indices, 16)
                            sp.dma_start(b[TFULL - TA:TFULL - TA + 1, 0:TREST],
                                         edges[TFULL * P:E].rearrange("(t e) -> t e", t=1)).then_inc(indices, 16)
                        for j in range(J):
                            sp.dma_start(WeB[DE * j:DE * (j + 1), D * j:D * (j + 1)], We[:, :]).then_inc(params, 16)
                            sp.dma_start(beB[0:1, D * j:D * (j + 1)], be.rearrange("(a d) -> a d", a=1)).then_inc(params, 16)
                        for w, t in ((W1, w1_raw), (W2, w2), (Wl, wl)):
                            sp.dma_start(t[:, :], w[:, :]).then_inc(params, 16)
                        sp.dma_start(blB[:, :], bl.rearrange("(a d) -> a d", a=1).broadcast_to((P, D))).then_inc(params, 16)
                        sp.dma_start(epst[:, :], epsilon.rearrange("(a d) -> a d", a=1).broadcast_to((P, 1))).then_inc(params, 16)
                        for n, v in enumerate((b1, g1, beta1, b2, g2, beta2, bl)):
                            sp.dma_start(cols[:, n:n + 1], v.rearrange("(p a) -> p a", a=1)).then_inc(params, 16)
                        sp.wait_ge(const, 9)
                        for t in (table, out):
                            sp.dma_start(t[N:ROWS, :].rearrange("(p r) d -> p (r d)", p=P), zeros[:, :]).then_inc(emptied, 16)
                        sp.wait_ge(emptied, 32)
                        sp.wait_ge(params, 16 * N_PARAMS)

                    @block.gpsimd
                    def _(pool):
                        pool.memset(idx_i[0][1][:, :], 0).then_inc(cleared, 1)
                        pool.memset(idx_i[1][1][:, :], 0).then_inc(cleared, 1)
                        pool.memset(WeB[:, :], 0.0).then_inc(cleared, 1)
                        pool.memset(ident[:, :], 0.0).then_inc(const, 1)
                        pool.memset(earlier[:, :], 1.0).then_inc(const, 1)
                        pool.memset(ones[:, :], 1.0).then_inc(const, 1)
                        pool.memset(zeros[:, :], 0.0).then_inc(const, 1)
                        pool.memset(lneps[:, :], EPS).then_inc(const, 1)
                        pool.iota(trash_i[:, :], pattern=[[P, J]], base=N, channel_multiplier=1).then_inc(const, 1)
                        pool.wait_ge(const, 6)
                        pool.affine_select(out=ident[:, :], in_=ident[:, :], compare_op=ALU.not_equal, fill=1.0,
                                           base=0, pattern=[[-1, P]], channel_multiplier=1).then_inc(const, 1)
                        pool.affine_select(out=earlier[:, GE - P:GE], in_=earlier[:, GE - P:GE], compare_op=ALU.is_gt,
                                           fill=0.0, base=0, pattern=[[-1, P]], channel_multiplier=1).then_inc(const, 1)
                        pool.tensor_copy(trash[:, :], trash_i[:, :]).then_inc(const, 1)
                        pool.wait_ge(turned, 2)
                        for t in (src_k, dst_k):
                            pool.affine_select(out=t[:, GFULL:NG, :], in_=t[:, GFULL:NG, :], compare_op=ALU.is_gt,
                                               fill=float(PAD), base=E - GFULL * GE,
                                               pattern=[[-GE, NG - GFULL], [-P, J]], channel_multiplier=-1).then_inc(keys, 1)

                    @block.vector
                    def _(dve):
                        dve.wait_ge(indices, 16 * 6)
                        for n in range(2):
                            for h in range(2):
                                dve.tensor_copy(idx_f[n][h][:, :], idx_i[n][h][:, :]).then_inc(rows_f, 1)
                        dve.wait_ge(keys, 4)
                        for n, (k, i) in enumerate(((src_k, src_i), (dst_k, dst_i))):
                            dve.tensor_copy(flat(i), psum[n][:, 0:NTILE]).then_inc(placed, 1)
                            dve.tensor_copy(flat(k), psum[n][:, 0:NTILE]).then_inc(turned, 1)
                        dve.wait_ge(params, 16 * N_PARAMS)
                        dve.memset(unit[:, :], 1.0).then_inc(sized, 1)
                        dve.memset(sign[:, 1:2], 1.0).then_inc(sized, 1)
                        dve.tensor_scalar(eps1[:, 0:1], epst[:, :], 1.0, None, ALU.add).then_inc(sized, 1)
                        dve.wait_ge(sized, 3)
                        dve.tensor_scalar(eps1[:, 1:2], eps1[:, 0:1], 0.0, None, ALU.is_lt).then_inc(sized, 1)
                        dve.wait_ge(sized, 4)
                        dve.tensor_scalar(sign[:, 0:1], eps1[:, 1:2], -2.0, 1.0, ALU.mult, ALU.add).then_inc(sized, 1)
                        dve.wait_ge(sized, 5)
                        dve.tensor_scalar(gain[:, :], unit[:, :], eps1[:, 0:1], sign[:, 0:1], ALU.mult, ALU.mult).then_inc(sized, 1)
                        dve.tensor_scalar(w1[:, :], w1_raw[:, :], sign[:, 0:1], None, ALU.mult).then_inc(sized, 1)
                        dve.wait_ge(wl_turned, 1)
                        dve.tensor_copy(wlT[:, :], psum[2][:, 0:D]).then_inc(placed, 1)

                    @block.tensor
                    def _(pe):
                        pe.wait_ge(const, 9)
                        pe.wait_ge(rows_f, 4)
                        for n in range(2):
                            for h, t in enumerate((TA, TB)):
                                nc.tensor.transpose(psum[n][:, h * P:h * P + t], idx_f[n][h][0:t, :], ident[0:t, 0:t]).then_inc(keys, 1)
                        pe.wait_ge(params, 16 * N_PARAMS)
                        nc.tensor.transpose(psum[2][:, 0:D], wl[:, :], ident[:, :]).then_inc(wl_turned, 1)

            n_xin = sems("n_xin", B); n_st = sem("n_st"); n_mv = sem("n_mv"); n_sd = sem("n_sd"); n_rs = sem("n_rs"); n_iv = sem("n_iv")
            n_nm = sem("n_nm"); n_h = sem("n_h"); n_out = sems("n_out", B)
            g_ea = sems("g_ea", 2); g_gi = sem("g_gi"); g_xs = sems("g_xs", 2); g_st = sem("g_st"); g_mv = sem("g_mv")
            g_sd = sem("g_sd"); g_rs = sem("g_rs"); g_h = sem("g_h"); g_msg = sem("g_msg")
            g_tp = sem("g_tp"); g_tc = sem("g_tc"); g_ef = sem("g_ef"); g_er = sem("g_er")
            with ExitStack() as scope:
                xb = ring("n_x", B, [P, C, D], f32, scope); hb = ring("n_h_", B, [P, C, D], f32, scope)
                st = ring("n_st_", B, [P, C, 6], f32, scope); mv = ring("n_mv_", B, [P, C, 2], f32, scope)
                sd = ring("n_sd_", B, [P, C], f32, scope); rs = ring("n_rs_", B, [P, C], f32, scope); nm = ring("n_nm_", B, [P, C], f32, scope)
                iv = ring("n_iv_", B, [P, C], f32, scope)
                gi = ring("g_i", 2, [P, J], i32, scope); xs = ring("g_x", 2, [P, J, D], f32, scope); hs = ring("g_hs", 2, [P, J, D], f32, scope)
                gst = ring("g_st_", 2, [P, J, 6], f32, scope); gmv = ring("g_mv_", 2, [P, J, 2], f32, scope)
                gsd = ring("g_sd_", 2, [P, J], f32, scope); grs = ring("g_rs_", 2, [P, J], f32, scope)
                ea = ring("g_ea_", 2, [P, J, DE], f32, scope); eaT = ring("g_eaT", 2, [J * DE, P], f32, scope)
                ef = ring("g_ef_", 2, [P, J, D], f32, scope)
                eaT_p = [psum[v][:, 0:P] for v in range(2)]
                ef_p = [psum[2 + v][:, 0:BANK] for v in range(2)]

                def turns(eng, block_step, group_step):
                    def step(i, u):
                        block_step(i, u)
                        if u % 2:
                            group_step(i, u // 2)
                    steps(eng, NB, B, step, B)
                    group_step((NG - 1) // 2, (NG - 1) % 2)

                with nc.Block() as block:
                    @block.sync
                    def _(sp):
                        def blocks(i, u):
                            k = B * i + u
                            wait(sp, n_h, k - B + 1)
                            sp.dma_start(flat(xb[u]), node_rows(x, k)).then_inc(n_xin[u], 16)
                            if inside(k - 3, NB):
                                store(*moved(i, u, -3, B))

                        def store(i, u):
                            k = B * i + u
                            wait(sp, n_h, k + 1)
                            lo = SEEN if tail(k) else 0
                            sp.dma_start(node_rows(table, k, lo), flat(hb[u][lo:P])).then_inc(n_out[u], 16)

                        def groups(i, v):
                            g = 2 * i + v
                            if isinstance(g, int) and g > GFULL:
                                return
                            wait(sp, g_tp, g - 1)
                            last = isinstance(g, int) and g == GFULL
                            n = TFULL - GFULL * J if last else J
                            sp.dma_start(ea[v][:, 0:n, :], edge_attr[bass.ds(GE * g, n * P), :].rearrange(
                                "(j p) d -> p j d", p=P)).then_inc(g_ea[v], 16)
                            if last:
                                sp.dma_start(ea[v][0:TREST, n, :], edge_attr[TFULL * P:E, :]).then_inc(g_ea[v], 16)
                        turns(sp, blocks, groups)
                        for k in range(NB - 3, NB):
                            store(k // B, k % B)
                        for u in range(B):
                            sp.wait_ge(n_out[u], 16 * ((NB - u + B - 1) // B))

                    @block.gpsimd
                    def _(pool):
                        def gather(i, v):
                            g = 2 * i + v
                            wait(pool, g_h, g - 1)
                            pool.sem_inc(pool_go, 1)
                            pool.tensor_copy(gi[v][:, :], kept(src_i, g)).then_inc(g_gi, 1)
                            wait(pool, g_gi, g + 1)
                            pool.sem_inc(pool_go, 1)
                            for j in range(J):
                                pool.indirect_dma_start(
                                    out=xs[v][:, j, :], out_offset=None, in_=x[:, :],
                                    in_offset=bass.IndirectOffsetOnAxis(ap=gi[v][:, j:j + 1], axis=0)).then_inc(g_xs[v], 16)
                        steps(pool, NG, 2, gather, 2)

                    @block.vector
                    def _(dve):
                        def stats(i, u):
                            k = B * i + u
                            wait(dve, n_xin[u], 16 * (i + 1))
                            for c in range(C):
                                dve.bn_stats(st[u][:, c, :], xb[u][:, c, :]).then_inc(n_st, 1)
                            wait(dve, n_st, C * (k + 1))
                            dve.sem_inc(dve_go, 1)
                            for c in range(C):
                                m = dve.bn_aggr(mv[u][:, c, :], st[u][:, c, :])
                            m.then_inc(n_mv, 1)

                        def invert(i, u):
                            k = B * i + u
                            wait(dve, n_sd, k + 1)
                            dve.reciprocal(iv[u][:, :], sd[u][:, :]).then_inc(n_iv, 1)
                            wait(dve, n_iv, k + 1)
                            dve.tensor_tensor(rs[u][:, :], gain[:, :], iv[u][:, :], ALU.mult).then_inc(n_rs, 1)
                            wait(dve, n_rs, k + 1)
                            dve.scalar_tensor_tensor(out=nm[u][:, :], in0=mv[u][:, :, 0], scalar=-1.0, in1=rs[u][:, :],
                                                     op0=ALU.mult, op1=ALU.mult).then_inc(n_nm, 1)

                        def blocks(i, u):
                            k = B * i + u
                            if inside(k + 1, NB):
                                invert(*moved(i, u, 1, B))
                            if inside(k + 2, NB):
                                stats(*moved(i, u, 2, B))

                        def group_stats(i, v):
                            g = 2 * i + v
                            wait(dve, g_xs[v], 16 * J * (i + 1))
                            for j in range(J):
                                dve.bn_stats(gst[v][:, j, :], xs[v][:, j, :]).then_inc(g_st, 1)
                            wait(dve, g_st, J * (g + 1))
                            dve.sem_inc(dve_go, 1)
                            for j in range(J):
                                m = dve.bn_aggr(gmv[v][:, j, :], gst[v][:, j, :])
                            m.then_inc(g_mv, 1)

                        def groups(i, v):
                            g = 2 * i + v
                            wait(dve, g_sd, g + 1)
                            dve.reciprocal(grs[v][:, :], gsd[v][:, :]).then_inc(g_rs, 1)
                            wait(dve, g_rs, g + 1)
                            for j in range(J):
                                m = dve.tensor_scalar(hs[v][:, j, :], xs[v][:, j, :], gmv[v][:, j, 0:1], grs[v][:, j:j + 1],
                                                      ALU.subtract, ALU.mult)
                            m.then_inc(g_h, 1)
                            wait(dve, g_h, g + 1)
                            wait(dve, g_er, g + 1)
                            dve.scalar_tensor_tensor(out=kept(msgs, g), in0=flat(hs[v]), scalar=0.0, in1=flat(ef[v]),
                                                     op0=ALU.max, op1=ALU.add).then_inc(g_msg, 1)
                            if inside(g + 1, NG):
                                group_stats(*moved(i, v, 1, 2))
                        stats(0, 0)
                        stats(0, 1)
                        invert(0, 0)
                        group_stats(0, 0)
                        turns(dve, blocks, groups)

                    @block.scalar
                    def _(act):
                        def root(i, u):
                            wait(act, n_mv, B * i + u + 1)
                            act.activation(sd[u][:, :], mv[u][:, :, 1], ACT.Sqrt, bias=lneps[:, 0:1]).then_inc(n_sd, 1)

                        def blocks(i, u):
                            k = B * i + u
                            wait(act, n_nm, k + 1)
                            wait(act, n_out[u], 16 * i)
                            for c in range(C):
                                a = act.activation(hb[u][:, c, :], xb[u][:, c, :], ACT.Relu, bias=nm[u][:, c:c + 1],
                                                   scale=rs[u][:, c:c + 1])
                            a.then_inc(n_h, 1)
                            if inside(k + 2, NB):
                                root(*moved(i, u, 2, B))

                        def group_root(i, v):
                            wait(act, g_mv, 2 * i + v + 1)
                            act.activation(gsd[v][:, :], gmv[v][:, :, 1], ACT.Sqrt, bias=lneps[:, 0:1]).then_inc(g_sd, 1)

                        def features(i, v):
                            g = 2 * i + v
                            wait(act, g_tp, g + 1)
                            act.activation(eaT[v][:, :], eaT_p[v], ACT.Copy).then_inc(g_tc, 1)
                            wait(act, g_ef, g + 1)
                            wait(act, g_msg, g - 1)
                            act.activation(flat(ef[v]), ef_p[v], ACT.Relu).then_inc(g_er, 1)

                        def groups(i, v):
                            g = 2 * i + v
                            if inside(g + 1, NG):
                                features(*moved(i, v, 1, 2))
                                group_root(*moved(i, v, 1, 2))
                        root(0, 0)
                        root(0, 1)
                        features(0, 0)
                        group_root(0, 0)
                        turns(act, blocks, groups)

                    @block.tensor
                    def _(pe):
                        def features(i, v):
                            g = 2 * i + v
                            if not (isinstance(g, int) and g > GFULL):
                                extra = 16 if isinstance(g, int) and g == GFULL else 0
                                wait(pe, g_ea[v], 16 * (i + 1) + extra)
                            wait(pe, g_tc, g - 1)
                            nc.tensor.transpose(eaT_p[v], flat(ea[v]), ident[:, :]).then_inc(g_tp, 1)
                            wait(pe, g_er, g - 1)
                            nc.tensor.matmul(ef_p[v], ones[0:1, :], beB[0:1, :], start=True, stop=False)
                            wait(pe, g_tc, g + 1)
                            nc.tensor.matmul(ef_p[v], eaT[v][:, :], WeB[:, :], start=False, stop=True).then_inc(g_ef, 1)
                        steps(pe, NG, 2, features, 2)

        def add_messages(name, target, ends, keys_f, layer, degrees):
            a_kin = sems(name + "_kin", R); a_same = sem(name + "_same"); a_cnt = sem(name + "_cnt")
            a_gap = sem(name + "_gap"); a_hop = sem(name + "_hop"); a_dest = sem(name + "_dest"); a_pad = sem(name + "_pad")
            a_tot = sem(name + "_tot"); a_pay = sem(name + "_pay"); a_sent = sems(name + "_sent", R)
            a_hot = sem(name + "_hot"); a_used = sem(name + "_used"); a_deg = sem(name + "_deg"); a_rt = sem(name + "_rt")
            a_dis = sem(name + "_dis"); a_iota = sem(name + "_iota"); a_half = sem(name + "_half")
            with ExitStack() as scope:
                kT = ring(name + "kT", R, [P, GE], i32, scope); same = ring(name + "same", R, [P, J, GE], f32, scope)
                junk = sb(name + "junk", [P, J, GE], f32, scope)
                count = ring(name + "count", R, [P, J], f32, scope); gap = ring(name + "gap", R, [P, J], f32, scope)
                hop = ring(name + "hop", R, [P, J], f32, scope); dest = ring(name + "dest", R, [P, J], i32, scope)
                pay = ring(name + "pay", R, [P, J, D], f32, scope)
                tot_p = [psum[2][:, 0:BANK], psum[2][:, BANK:2 * BANK], psum[3][:, 0:BANK]]
                if degrees:
                    RW = HALVES * P
                    iota_i = sb("iota_i", [P, QW], i32, scope); iota_f = sb("iota_f", [P, QW], f32, scope)
                    key_i = sb("key_i", [P, NTILE], i32, scope); half_i = ring("half_i", 2, [P, NTILE], i32, scope)
                    half_f = ring("half_f", 2, [P, NTILE], f32, scope)
                    hot_r = ring("hot_r", J, [P, RW], bf16, scope); hot_c = ring("hot_c", J, [P, QW], bf16, scope)
                    deg = sb("deg", [P, HALVES * QW], f32, scope); root = sb("root", [P, HALVES * QW], f32, scope)
                    inv = sb("inv", [P, HALVES * QW], f32, scope)
                    assert HALVES == 2 and QW == BANK
                    deg_p = psum[0][:, :]

                with nc.Block() as block:
                    @block.sync
                    def _(sp):
                        def load(i, u):
                            k = R * i + u
                            if isinstance(k, int) and k > GFULL:
                                return
                            n = E - GFULL * GE if isinstance(k, int) and k == GFULL else GE
                            wait(sp, a_same, J * (k - R + 1))
                            sp.dma_start(kT[u][:, 0:n], ends[bass.ds(GE * k, n)].rearrange(
                                "(a e) -> a e", a=1).broadcast_to((P, n))).then_inc(a_kin[u], 16)
                        steps(sp, NG, R, load, 2)
                        if degrees:
                            sp.wait_ge(a_dis, 2)
                            for h in range(HALVES):
                                sp.dma_start(dis_tab[h * P * QW:(h + 1) * P * QW, :].rearrange("(p q) a -> p (q a)", q=QW),
                                             inv[:, h * QW:(h + 1) * QW]).then_inc(a_dis, 16)
                            sp.wait_ge(a_dis, 2 + 16 * HALVES)

                    @block.gpsimd
                    def _(pool):
                        if degrees:
                            pool.iota(iota_i[:, :], pattern=[[1, QW]], base=0, channel_multiplier=0).then_inc(a_iota, 1)
                            pool.wait_ge(a_iota, 1)
                            pool.tensor_copy(iota_f[:, :], iota_i[:, :]).then_inc(a_iota, 1)

                        def add(i, u):
                            k = R * i + u
                            wait(pool, a_pay, k + 1)
                            wait(pool, a_dest, k + 1)
                            wait(pool, a_sent[(u - 1) % R], 16 * J * (i + (u + 2) // R))
                            pool.sem_inc(pool_go, 1)
                            for j in range(J):
                                pool.indirect_dma_start(
                                    out=target[:, :], out_offset=bass.IndirectOffsetOnAxis(ap=dest[u][:, j:j + 1], axis=0),
                                    in_=pay[u][:, j, :], in_offset=None, compute_op=ALU.add).then_inc(a_sent[u], 16)
                        steps(pool, NG, R, add, 1)
                        for u in range(R):
                            pool.wait_ge(a_sent[u], 16 * J * ((NG - u + R - 1) // R))

                    @block.vector
                    def _(dve):
                        def places(i, u):
                            k = R * i + u
                            if isinstance(k, int) and k >= GFULL:
                                n = E - GFULL * GE if k == GFULL else 0
                                dve.memset(kT[u][:, n:GE], PAD).then_inc(a_pad, 1)
                                dve.wait_ge(a_pad, k - GFULL + 1)
                            if not (isinstance(k, int) and k > GFULL):
                                wait(dve, a_kin[u], 16 * (i + 1))
                            wait(dve, a_tot, k - R + 1)
                            for j in range(J):
                                dve.tensor_scalar(same[u][:, j, :], kT[u][:, :], keys_f[:, bass.ds(k, 1), j],
                                                  sign[:, layer:layer + 1], ALU.is_equal, ALU.mult).then_inc(a_same, 1)
                            for j in range(J):
                                wait(dve, a_same, J * k + j + 1)
                                dve.tensor_tensor_reduce(out=junk[:, j, 0:(j + 1) * P], in0=same[u][:, j, 0:(j + 1) * P],
                                                         in1=earlier[:, GE - (j + 1) * P:GE], scale=1.0, scalar=0.0,
                                                         op0=ALU.mult, op1=ALU.add,
                                                         accum_out=count[u][:, j:j + 1]).then_inc(a_cnt, 1)
                            wait(dve, a_sent[u], 16 * J * i)
                            dve.tensor_tensor(gap[u][:, :], trash[:, :], kept(keys_f, k), ALU.subtract).then_inc(a_gap, 1)
                            if degrees:
                                one_hots(k)
                            wait(dve, a_gap, k + 1)
                            wait(dve, a_cnt, J * (k + 1))
                            dve.scalar_tensor_tensor(out=hop[u][:, :], in0=count[u][:, :], scalar=0.0, in1=gap[u][:, :],
                                                     op0=ALU.not_equal, op1=ALU.mult).then_inc(a_hop, 1)
                            wait(dve, a_hop, k + 1)
                            dve.tensor_tensor(dest[u][:, :], hop[u][:, :], kept(keys_f, k), ALU.add).then_inc(a_dest, 1)

                        def one_hots(k):
                            wait(dve, a_used, J * k)
                            for j in range(J):
                                dve.tensor_scalar(hot_r[j][:, :], iota_f[:, 0:RW], half_f[0][:, bass.ds(J * k + j, 1)], None, ALU.is_equal).then_inc(a_hot, 1)
                                dve.tensor_scalar(hot_c[j][:, :], iota_f[:, :], half_f[1][:, bass.ds(J * k + j, 1)], None, ALU.is_equal).then_inc(a_hot, 1)

                        if degrees:
                            dve.tensor_copy(key_i[:, :], flat(src_k)).then_inc(a_half, 1)
                            dve.wait_ge(a_half, 1)
                            dve.tensor_scalar(half_i[0][:, :], key_i[:, :], QB, None, ALU.logical_shift_right).then_inc(a_half, 1)
                            dve.tensor_scalar(half_i[1][:, :], key_i[:, :], QW - 1, None, ALU.bitwise_and).then_inc(a_half, 1)
                            dve.wait_ge(a_half, 3)
                            dve.tensor_copy(half_f[0][:, :], half_i[0][:, :]).then_inc(a_half, 1)
                            dve.tensor_copy(half_f[1][:, :], half_i[1][:, :]).then_inc(a_half, 1)
                            dve.wait_ge(a_half, 5)
                            dve.wait_ge(a_iota, 2)
                        steps(dve, NG, R, places, 2)
                        if degrees:
                            dve.wait_ge(a_used, NTILE)
                            dve.tensor_scalar(deg[:, :], deg_p, 1.0, None, ALU.max).then_inc(a_deg, 1)
                            dve.wait_ge(a_rt, 1)
                            dve.reciprocal(inv[:, :], root[:, :]).then_inc(a_dis, 1)
                            dve.wait_ge(a_dis, 1)
                            dve.scalar_tensor_tensor(out=inv[:, :], in0=deg_p, scalar=0.0, in1=inv[:, :],
                                                     op0=ALU.is_gt, op1=ALU.mult).then_inc(a_dis, 1)

                    @block.tensor
                    def _(pe):
                        def sums(i, u):
                            k = R * i + u
                            wait(pe, a_same, J * (k + 1))
                            wait(pe, a_pay, k - R + 1)
                            rows = kept(msgs, k)
                            for o in range(J):
                                for j in range(J):
                                    m = nc.tensor.matmul(tot_p[u][:, o * D:(o + 1) * D], same[u][:, j, o * P:(o + 1) * P],
                                                         rows[:, j * D:(j + 1) * D], start=(j == 0), stop=(j == J - 1))
                            m.then_inc(a_tot, 1)
                            if degrees:
                                for j in range(J):
                                    first = isinstance(k, int) and k == 0 and j == 0
                                    final = isinstance(k, int) and k == NG - 1 and j == J - 1
                                    wait(pe, a_hot, 2 * (J * k + j + 1))
                                    for h in range(HALVES):
                                        m = nc.tensor.matmul(psum[0][:, h * QW:(h + 1) * QW], hot_r[j][:, h * P:(h + 1) * P],
                                                             hot_c[j][:, :], start=first, stop=final)
                                    m.then_inc(a_used, 1)
                        steps(pe, NG, R, sums, 1)

                    @block.scalar
                    def _(act):
                        def keep(i, u):
                            k = R * i + u
                            wait(act, a_tot, k + 1)
                            wait(act, a_sent[u], 16 * J * i)
                            act.activation(flat(pay[u]), tot_p[u], ACT.Copy).then_inc(a_pay, 1)
                        steps(act, NG, R, keep, 1)
                        if degrees:
                            act.wait_ge(a_deg, 1)
                            act.activation(root[:, :], deg[:, :], ACT.Sqrt).then_inc(a_rt, 1)

        add_messages("s", table, dst, dst_k, 0, True)

        def stat_slices(k, y):
            if tail(k):
                return [(2 * (NB - 1) + c, y[:, c * P + SEEN:(c + 1) * P]) for c in range(C)]
            return [(2 * k + h, y[:, h * BANK:(h + 1) * BANK]) for h in range(2)]

        def take_stats(dve, k, y):
            for n, part in stat_slices(k, y):
                m = dve.bn_stats(kept(stat, n), part)
            return m

        bn_chain = sem("bn_chain"); bn_root = sem("bn_root")

        def batch_norm(dve, n, mvt, tmp):
            b, g, beta = (cols[:, 3 * n + m:3 * n + m + 1] for m in range(3))

            def link(ins, m):
                ins.then_inc(bn_chain, 1)
                dve.wait_ge(bn_chain, 6 * n + m)
            link(dve.bn_aggr(mvt[:, 0:2], flat(stat)), 1)
            dve.wait_ge(bn_root, n + 1)
            link(dve.reciprocal(tmp[:, 1:2], tmp[:, 0:1]), 2)
            link(dve.tensor_tensor(bn_s[:, n:n + 1], g, tmp[:, 1:2], ALU.mult), 3)
            link(dve.tensor_tensor(tmp[:, 2:3], mvt[:, 0:1], b, ALU.add), 4)
            link(dve.tensor_tensor(tmp[:, 3:4], b, tmp[:, 2:3], ALU.subtract), 5)
            link(dve.scalar_tensor_tensor(out=bn_t[:, n:n + 1], in0=tmp[:, 3:4], scalar=bn_s[:, n:n + 1], in1=beta,
                                          op0=ALU.mult, op1=ALU.add), 6)

        def bn_square_root(act, n, mvt, tmp):
            act.wait_ge(bn_chain, 6 * n + 1)
            act.activation(tmp[:, 0:1], mvt[:, 1:2], ACT.Sqrt, bias=lneps[:, 0:1]).then_inc(bn_root, 1)

        def in_sbuf(u):
            return u == B - 1

        p1_in = sems("p1_in", B); p1_tp = sem("p1_tp"); p1_hT = sem("p1_hT"); p1_y = sem("p1_y"); p1_bn = sem("p1_bn")
        p1_ev = sem("p1_ev"); p1_out = sems("p1_out", B)
        with ExitStack() as scope:
            hb = ring("p1_h", B, [P, C, D], f32, scope); hT = ring("p1_hT_", 2, [P, BN], f32, scope)
            yb = ring("p1_y_", B - 1, [P, BN], f32, scope)
            mvt = sb("mvt1", [P, 2], f32, scope); tmp = sb("tmp1", [P, 4], f32, scope)

            with nc.Block() as block:
                @block.sync
                def _(sp):
                    def load(i, u):
                        k = B * i + u
                        wait(sp, p1_tp, k - B + 1)
                        sp.dma_start(flat(hb[u]), node_rows(table, k)).then_inc(p1_in[u], 16)
                        if inside(k - 3, NB):
                            store(*moved(i, u, -3, B))

                    def store(i, u):
                        k = B * i + u
                        if in_sbuf(u):
                            return
                        wait(sp, p1_ev, k + 1)
                        sp.dma_start(spilled(y1_s, k), yb[u][:, :]).then_inc(p1_out[u], 16)
                    steps(sp, NB, B, load, 2)
                    for k in range(NB - 3, NB):
                        store(k // B, k % B)
                    for u in range(B - 1):
                        sp.wait_ge(p1_out[u], 16 * ((NB - u + B - 1) // B))

                @block.tensor
                def _(pe):
                    def turn(i, u):
                        k = B * i + u
                        wait(pe, p1_in[u], 16 * (i + 1))
                        wait(pe, p1_hT, k - 1)
                        for c in range(C):
                            m = nc.tensor.transpose(psum[u % 2][:, c * P:(c + 1) * P], hb[u][:, c, :], ident[:, :])
                        m.then_inc(p1_tp, 1)

                    def step(i, u):
                        k = B * i + u
                        if inside(k + 1, NB):
                            turn(*moved(i, u, 1, B))
                        wait(pe, p1_hT, k + 1)
                        wait(pe, p1_ev, k - 1)
                        for h in range(2):
                            m = nc.tensor.matmul(psum[2 + u % 2][:, h * BANK:(h + 1) * BANK], w1[:, :],
                                                 hT[u % 2][:, h * BANK:(h + 1) * BANK], start=True, stop=True)
                        m.then_inc(p1_y, 1)
                    turn(0, 0)
                    steps(pe, NB, B, step, 2)

                @block.scalar
                def _(act):
                    def step(i, u):
                        k = B * i + u
                        wait(act, p1_tp, k + 1)
                        wait(act, p1_y, k - 1)
                        act.activation(hT[u % 2][:, :], psum[u % 2][:, :], ACT.Copy).then_inc(p1_hT, 1)
                    steps(act, NB, B, step, 2)
                    bn_square_root(act, 0, mvt, tmp)

                @block.vector
                def _(dve):
                    def step(i, u):
                        k = B * i + u
                        wait(dve, p1_y, k + 1)
                        take_stats(dve, k, psum[2 + u % 2]).then_inc(p1_bn, 1)
                        if in_sbuf(u):
                            y = kept(ykept, i)
                        else:
                            y = yb[u][:, :]
                            wait(dve, p1_out[u], 16 * i)
                        dve.tensor_copy(y, psum[2 + u % 2][:, :]).then_inc(p1_ev, 1)
                    steps(dve, NB, B, step, 2)
                    dve.wait_ge(p1_bn, NB)
                    batch_norm(dve, 0, mvt, tmp)

        d_idx = sem("d_idx"); d_got = sem("d_got"); d_kept = sem("d_kept")

        def gather_degrees(pool, n, ends, gi, gv):
            def group(k):
                m = NG * n + k
                wait(pool, d_kept, m)
                pool.sem_inc(pool_go, 1)
                pool.tensor_copy(gi[:, :], kept(ends, k)).then_inc(d_idx, 1)
                wait(pool, d_idx, m + 1)
                pool.sem_inc(pool_go, 1)
                for j in range(J):
                    pool.indirect_dma_start(
                        out=gv[:, j:j + 1], out_offset=None, in_=dis_tab[:, :],
                        in_offset=bass.IndirectOffsetOnAxis(ap=gi[:, j:j + 1], axis=0)).then_inc(d_got, 16)
                wait(pool, d_got, 16 * J * (m + 1))
                pool.sem_inc(pool_go, 1)
                pool.tensor_copy(kept(norm[n], k), gv[:, :]).then_inc(d_kept, 1)
            group(0)
            with pool.Fori(1, NG) as k:
                group(k)

        p2_in = sems("p2_in", B); p2_z = sem("p2_z"); p2_y = sem("p2_y"); p2_bn = sem("p2_bn"); p2_ev = sems("p2_ev", 2)
        p2_out = sems("p2_out", B)
        with ExitStack() as scope:
            ub = ring("p2_u", B - 1, [P, BN], f32, scope); z1 = ring("p2_z_", 2, [P, BN], f32, scope)
            vb = ring("p2_v", B - 1, [P, BN], f32, scope)
            mvt = sb("mvt2", [P, 2], f32, scope); tmp = sb("tmp2", [P, 4], f32, scope)
            gi = sb("p2_gi", [P, J], i32, scope); gv = sb("p2_gv", [P, J], f32, scope)

            with nc.Block() as block:
                @block.sync
                def _(sp):
                    def load(i, u):
                        k = B * i + u
                        if not in_sbuf(u):
                            wait(sp, p2_z, k - B + 1)
                            sp.dma_start(ub[u][:, :], spilled(y1_s, k)).then_inc(p2_in[u], 16)
                        if inside(k - 3, NB):
                            store(*moved(i, u, -3, B))

                    def store(i, u):
                        k = B * i + u
                        if in_sbuf(u):
                            return
                        wait(sp, p2_ev[u % 2], 2 * i + u // 2 + 1)
                        sp.dma_start(spilled(y2_s, k), vb[u][:, :]).then_inc(p2_out[u], 16)
                    steps(sp, NB, B, load, 2)
                    for k in range(NB - 3, NB):
                        store(k // B, k % B)
                    for u in range(B - 1):
                        sp.wait_ge(p2_out[u], 16 * ((NB - u + B - 1) // B))

                @block.gpsimd
                def _(pool):
                    gather_degrees(pool, 0, src_i, gi, gv)

                @block.scalar
                def _(act):
                    def step(i, u):
                        k = B * i + u
                        if in_sbuf(u):
                            y = kept(ykept, i)
                        else:
                            wait(act, p2_in[u], 16 * (i + 1))
                            y = ub[u][:, :]
                        wait(act, p2_y, k - 1)
                        act.activation(z1[u % 2][:, :], y, ACT.Relu, bias=bn_t[:, 0:1], scale=bn_s[:, 0:1]).then_inc(p2_z, 1)
                        if u % 2 == 1 and inside(k - 3, NB):
                            keep(*moved(i, u, -3, B))

                    def keep(i, u):
                        k = B * i + u
                        wait(act, p2_bn, k + 1)
                        wait(act, p2_out[u], 16 * i)
                        act.activation(vb[u][:, :], psum[u][:, :], ACT.Copy).then_inc(p2_ev[0], 1)
                    steps(act, NB, B, step, 2)
                    keep((NB - 2) // B, (NB - 2) % B)
                    bn_square_root(act, 1, mvt, tmp)

                @block.tensor
                def _(pe):
                    def step(i, u):
                        k = B * i + u
                        wait(pe, p2_z, k + 1)
                        wait(pe, p2_ev[u % 2], 2 * (i - 1) + u // 2 + 1)
                        for h in range(2):
                            m = nc.tensor.matmul(psum[u][:, h * BANK:(h + 1) * BANK], w2[:, :],
                                                 z1[u % 2][:, h * BANK:(h + 1) * BANK], start=True, stop=True)
                        m.then_inc(p2_y, 1)
                    steps(pe, NB, B, step, 2)

                @block.vector
                def _(dve):
                    def step(i, u):
                        k = B * i + u
                        wait(dve, p2_y, k + 1)
                        take_stats(dve, k, psum[u]).then_inc(p2_bn, 1)
                        if u % 2 == 0:
                            return
                        if in_sbuf(u):
                            y = kept(ykept, i)
                        else:
                            y = vb[u][:, :]
                            wait(dve, p2_out[u], 16 * i)
                        dve.tensor_copy(y, psum[u][:, :]).then_inc(p2_ev[1], 1)
                    steps(dve, NB, B, step, 2)
                    dve.wait_ge(p2_bn, NB)
                    batch_norm(dve, 1, mvt, tmp)

        p3_in = sems("p3_in", B); p3_xin = sems("p3_xin", B); p3_z = sem("p3_z"); p3_zb = sem("p3_zb"); p3_tp = sem("p3_tp")
        p3_x2 = sem("p3_x2"); p3_out = sems("p3_out", B)
        with ExitStack() as scope:
            yb = ring("p3_y", B - 1, [P, BN], f32, scope); xb = ring("p3_x", B, [P, C, D], f32, scope)
            zb = ring("p3_z_", 2, [P, BN], f32, scope); ob = ring("p3_o", 2, [P, C, D], f32, scope)
            gi = sb("p3_gi", [P, J], i32, scope); gv = sb("p3_gv", [P, J], f32, scope)

            with nc.Block() as block:
                @block.sync
                def _(sp):
                    def load(i, u):
                        k = B * i + u
                        if not in_sbuf(u):
                            wait(sp, p3_z, k - B + 1)
                            sp.dma_start(yb[u][:, :], spilled(y2_s, k)).then_inc(p3_in[u], 16)
                        wait(sp, p3_x2, k - B + 1)
                        sp.dma_start(flat(xb[u]), node_rows(x, k)).then_inc(p3_xin[u], 16)
                        if inside(k - 3, NB):
                            store(*moved(i, u, -3, B))

                    def store(i, u):
                        k = B * i + u
                        wait(sp, p3_x2, k + 1)
                        lo = SEEN if tail(k) else 0
                        sp.dma_start(node_rows(out, k, lo), flat(ob[u % 2][lo:P])).then_inc(p3_out[u], 16)
                    steps(sp, NB, B, load, 2)
                    for k in range(NB - 3, NB):
                        store(k // B, k % B)
                    for u in range(B):
                        sp.wait_ge(p3_out[u], 16 * ((NB - u + B - 1) // B))

                @block.gpsimd
                def _(pool):
                    gather_degrees(pool, 1, dst_i, gi, gv)

                @block.scalar
                def _(act):
                    def step(i, u):
                        k = B * i + u
                        if in_sbuf(u):
                            y = kept(ykept, i)
                        else:
                            wait(act, p3_in[u], 16 * (i + 1))
                            y = yb[u][:, :]
                        wait(act, p3_tp, k - 1)
                        act.activation(zb[u % 2][:, :], y, ACT.Relu, bias=bn_t[:, 1:2], scale=bn_s[:, 1:2]).then_inc(p3_z, 1)
                    steps(act, NB, B, step, 2)

                @block.tensor
                def _(pe):
                    def step(i, u):
                        k = B * i + u
                        wait(pe, p3_zb, k + 1)
                        wait(pe, p3_x2, k - 3)
                        for c in range(C):
                            m = nc.tensor.transpose(psum[u][:, c * P:(c + 1) * P], zb[u % 2][:, c * P:(c + 1) * P], ident[:, :])
                        m.then_inc(p3_tp, 1)
                    steps(pe, NB, B, step, 2)

                @block.vector
                def _(dve):
                    def bias(i, u):
                        k = B * i + u
                        wait(dve, p3_z, k + 1)
                        dve.tensor_scalar(zb[u % 2][:, :], zb[u % 2][:, :], cols[:, 6:7], None, ALU.add).then_inc(p3_zb, 1)

                    def step(i, u):
                        k = B * i + u
                        if inside(k + 1, NB):
                            bias(*moved(i, u, 1, B))
                        wait(dve, p3_tp, k + 1)
                        wait(dve, p3_xin[u], 16 * (i + 1))
                        before = moved(i, u, -2, B) if not isinstance(i, int) or k >= 2 else None
                        if before:
                            wait(dve, p3_out[before[1]], 16 * (before[0] + 1))
                        dve.tensor_tensor(flat(ob[u % 2]), psum[u][:, :], flat(xb[u]), ALU.add).then_inc(p3_x2, 1)
                    bias(0, 0)
                    steps(dve, NB, B, step, 2)

        m_gi = sem("m_gi"); m_xs = sems("m_xs", R); m_x2 = sem("m_x2"); m_st = sem("m_st"); m_mv = sem("m_mv"); m_sd = sem("m_sd")
        m_rs = sem("m_rs"); m_nm = sem("m_nm"); m_h = sem("m_h"); m_tp = sem("m_tp"); m_hT = sem("m_hT"); m_w = sem("m_w"); m_msg = sem("m_msg")
        m_norm = sem("m_norm")
        with ExitStack() as scope:
            gi = ring("m_gi_", R, [P, J], i32, scope); xs = ring("m_xs_", R, [P, J, D], f32, scope)
            x2 = ring("m_x2_", R, [P, J, D], f32, scope)
            st = ring("m_st_", R, [P, J, 6], f32, scope); mv = ring("m_mv_", R, [P, J, 2], f32, scope); sd = ring("m_sd_", R, [P, J], f32, scope)
            rs = ring("m_rs_", R, [P, J], f32, scope); nm = ring("m_nm_", R, [P, J], f32, scope)
            hs = ring("m_hs_", R, [P, J, D], f32, scope); hT = ring("m_hT_", R, [P, GE], f32, scope)
            hT_p = [psum[0][:, 0:BANK], psum[0][:, BANK:2 * BANK], psum[1][:, 0:BANK]]
            w_p = [psum[2][:, 0:BANK], psum[2][:, BANK:2 * BANK], psum[3][:, 0:BANK]]

            with nc.Block() as block:
                @block.gpsimd
                def _(pool):
                    def gather(i, u):
                        k = R * i + u
                        wait(pool, m_x2, k - R + 1)
                        pool.sem_inc(pool_go, 1)
                        pool.tensor_copy(gi[u][:, :], kept(dst_i, k)).then_inc(m_gi, 1)
                        wait(pool, m_gi, k + 1)
                        pool.sem_inc(pool_go, 1)
                        for j in range(J):
                            pool.indirect_dma_start(
                                out=xs[u][:, j, :], out_offset=None, in_=out[:, :],
                                in_offset=bass.IndirectOffsetOnAxis(ap=gi[u][:, j:j + 1], axis=0)).then_inc(m_xs[u], 16)
                    steps(pool, NG, R, gather, 1)

                @block.vector
                def _(dve):
                    def stats(i, u):
                        k = R * i + u
                        wait(dve, m_xs[u], 16 * J * (i + 1))
                        wait(dve, m_h, k - R + 1)
                        dve.tensor_tensor(x2[u][:, :, :], xs[u][:, :, :], blB[:, :].rearrange("p (a d) -> p a d", a=1).broadcast_to((P, J, D)),
                                          ALU.subtract).then_inc(m_x2, 1)
                        wait(dve, m_x2, k + 1)
                        for j in range(J):
                            dve.bn_stats(st[u][:, j, :], x2[u][:, j, :]).then_inc(m_st, 1)
                        wait(dve, m_st, J * (k + 1))
                        dve.sem_inc(dve_go, 1)
                        for j in range(J):
                            m = dve.bn_aggr(mv[u][:, j, :], st[u][:, j, :])
                        m.then_inc(m_mv, 1)

                    def invert(i, u):
                        k = R * i + u
                        wait(dve, m_sd, k + 1)
                        dve.reciprocal(rs[u][:, :], sd[u][:, :]).then_inc(m_rs, 1)
                        wait(dve, m_rs, k + 1)
                        dve.scalar_tensor_tensor(out=nm[u][:, :], in0=mv[u][:, :, 0], scalar=-1.0, in1=rs[u][:, :],
                                                 op0=ALU.mult, op1=ALU.mult).then_inc(m_nm, 1)

                    def weigh(i, u):
                        k = R * i + u
                        wait(dve, m_w, k + 1)
                        dve.tensor_tensor(msgs[:, bass.ds(k, 1), :].rearrange("p a (j d) -> p (a j) d", j=J),
                                          w_p[u].rearrange("p (j d) -> p j d", j=J),
                                          norm[0][:, bass.ds(k, 1), :].rearrange("p a j -> p j a").broadcast_to((P, J, D)),
                                          ALU.mult).then_inc(m_msg, 1)

                    def step(i, u):
                        k = R * i + u
                        if inside(k + 1, NG):
                            invert(*moved(i, u, 1, R))
                        if inside(k - 1, NG):
                            weigh(*moved(i, u, -1, R))
                        if inside(k + 2, NG):
                            stats(*moved(i, u, 2, R))
                    dve.tensor_tensor(norm[0][:, :, :], norm[0][:, :, :], norm[1][:, :, :], ALU.mult).then_inc(m_norm, 1)
                    dve.wait_ge(m_norm, 1)
                    stats(0, 0)
                    stats(0, 1)
                    invert(0, 0)
                    steps(dve, NG, R, step, 2)
                    weigh((NG - 1) // R, (NG - 1) % R)

                @block.scalar
                def _(act):
                    def root(i, u):
                        wait(act, m_mv, R * i + u + 1)
                        act.activation(sd[u][:, :], mv[u][:, :, 1], ACT.Sqrt, bias=lneps[:, 0:1]).then_inc(m_sd, 1)

                    def relu(i, u):
                        k = R * i + u
                        wait(act, m_nm, k + 1)
                        wait(act, m_tp, k - R + 1)
                        for j in range(J):
                            a = act.activation(hs[u][:, j, :], x2[u][:, j, :], ACT.Relu, bias=nm[u][:, j:j + 1],
                                               scale=rs[u][:, j:j + 1])
                        a.then_inc(m_h, 1)

                    def step(i, u):
                        k = R * i + u
                        wait(act, m_tp, k + 1)
                        wait(act, m_w, k - R + 1)
                        act.activation(hT[u][:, :], hT_p[u], ACT.Copy).then_inc(m_hT, 1)
                        if inside(k + 1, NG):
                            relu(*moved(i, u, 1, R))
                        if inside(k + 2, NG):
                            root(*moved(i, u, 2, R))
                    root(0, 0)
                    root(0, 1)
                    relu(0, 0)
                    steps(act, NG, R, step, 2)

                @block.tensor
                def _(pe):
                    def turn(i, u):
                        k = R * i + u
                        wait(pe, m_h, k + 1)
                        wait(pe, m_hT, k - R + 1)
                        for j in range(J):
                            m = nc.tensor.transpose(hT_p[u][:, j * P:(j + 1) * P], hs[u][:, j, :], ident[:, :])
                        m.then_inc(m_tp, 1)

                    def step(i, u):
                        k = R * i + u
                        wait(pe, m_hT, k + 1)
                        wait(pe, m_msg, k - R + 1)
                        for j in range(J):
                            m = nc.tensor.matmul(w_p[u][:, j * D:(j + 1) * D], hT[u][:, j * P:(j + 1) * P], wlT[:, :], start=True, stop=True)
                        m.then_inc(m_w, 1)
                        if inside(k + 1, NG):
                            turn(*moved(i, u, 1, R))
                    turn(0, 0)
                    steps(pe, NG, R, step, 1)

        add_messages("t", out, src, src_k, 1, False)


_INS = ['x', 'src', 'dst', 'edge_attr_32', 'L0_gnn_epsilon', 'L0_gnn_We', 'L0_gnn_be', 'L0_gnn_W1', 'L0_gnn_b1',
        'L0_gnn_g1', 'L0_gnn_beta1', 'L0_gnn_W2', 'L0_gnn_b2', 'L0_gnn_g2', 'L0_gnn_beta2', 'L1_gnn_W', 'L1_gnn_b']
_TRASH = 5 * 128


def kernel(**inputs):
    import numpy as _np
    import concourse.bacc as _bacc
    from concourse import mybir as _mybir
    from concourse.bass_utils import run_bass_kernel_spmd as _run

    nc = _bacc.Bacc("TRN2", target_bir_lowering=False, num_devices=1)
    arrays, args = {}, []
    for name in _INS:
        a = _np.ascontiguousarray(inputs[name])
        arrays[f"in_{name}_dram"] = a
        args.append(nc.dram_tensor(f"in_{name}_dram", a.shape, _mybir.dt.from_np(a.dtype), kind="ExternalInput").ap())
    n, d = inputs["x"].shape
    args.append(nc.dram_tensor("out_0_dram", (n + _TRASH, d), _mybir.dt.float32, kind="ExternalOutput").ap())
    preln_gin_then_gcn(nc, *args)
    r = _run(nc, [arrays], core_ids=[0])
    return r.results[0]["out_0_dram"][:n]
```

```python
import concourse.bass as bass
from concourse import mybir
from contextlib import ExitStack


def preln_gin_then_gcn(nc, x, src, dst, edge_attr, epsilon, We, be, W1, b1, g1, beta1,
                       W2, b2, g2, beta2, Wl, bl, out):
    f32, f16, i32 = mybir.dt.float32, mybir.dt.float16, mybir.dt.int32
    ALU = mybir.AluOpType
    ACT = mybir.ActivationFunctionType

    N, D = x.shape
    E, DE = edge_attr.shape
    P = 128
    J = 4
    GE = P * J
    NG = 2 * -(-E // (2 * GE))
    NTILE = NG * J
    G1, G2 = 5, 8
    GFULL = E // GE
    TFULL = E // P
    TREST = E - TFULL * P
    C = 8
    BN = P * C
    NB = -(-N // BN)
    TAIL = N - BN
    SEEN = ((NB - 1) * BN - TAIL) // C
    CN = 2 * C
    NBIG = -(-N // (P * CN))
    SEEN_BIG = (NBIG * P * CN - N) // CN
    BANK = 512
    PAD = N + G2 * P
    ROWS = out.shape[0]
    EPS = 1e-5
    QB = 9
    QW = 1 << QB
    HALVES = -(-(PAD + 1) // (QW * P))
    B = 6
    KEPT = (2, 5)
    SPILT = [u for u in range(B) if u not in KEPT]
    NKEPT = NB // B * len(KEPT)
    CUT = 34
    LAG = 4
    R = 3
    assert NB % B == 2 and NG == NBIG + 1 and (NBIG * P * CN - N) % CN == 0
    assert ROWS > PAD and (ROWS - N) % P == 0 and NG - 2 == GFULL and TREST > 0 and G1 <= G2
    assert ((NB - 1) * BN - TAIL) % C == 0 and TFULL // J == GFULL

    table = nc.dram_tensor("gin_input", (ROWS, D), f32, kind="Internal").ap()
    dis_tab = nc.dram_tensor("inv_sqrt_degree", (HALVES * P * QW, 1), f32, kind="Internal").ap()
    y1_s = nc.dram_tensor("y1_feature_major", (NB, P, BN), f32, kind="Internal").ap()

    def wait(eng, sem, value):
        if not (isinstance(value, int) and value <= 0):
            eng.wait_ge(sem, value)

    def steps(eng, n, ring, step, last, turns=1):
        full = (n - last) // ring
        for k in range(turns * ring):
            step(k // ring, k % ring)
        with eng.Fori(turns, full) as i:
            for u in range(ring):
                step(i, u)
        for k in range(full * ring, n):
            step(k // ring, k % ring)

    def moved(i, u, by, ring):
        return i + (u + by) // ring, (u + by) % ring

    def inside(k, n):
        return not isinstance(k, int) or 0 <= k < n

    def tail(k):
        return isinstance(k, int) and k == NB - 1

    def node_rows(t, k, lo=0):
        base = TAIL if tail(k) else BN * k
        return t[bass.ds(base + lo * C, (P - lo) * C), :].rearrange("(p c) d -> p (c d)", c=C)

    def kept(t, k):
        return t[:, bass.ds(k, 1), :].rearrange("p a f -> p (a f)")

    def spilled(t, k):
        return t[bass.ds(k, 1), :, :].rearrange("a p f -> p (a f)")

    def flat(t):
        return t[:, :, :].rearrange("p a f -> p (a f)")

    ctx = ExitStack()
    with ctx:
        def sem(name):
            return ctx.enter_context(nc.semaphore(name))

        def sems(name, n):
            return [sem(f"{name}{m}") for m in range(n)]

        def spilt_sems(name):
            return {u: sem(f"{name}{u}") for u in SPILT}

        def sb(name, shape, dt=f32, scope=ctx):
            return scope.enter_context(nc.sbuf_tensor(name, shape, dt))

        def ring(name, n, shape, dt=f32, scope=ctx):
            return [sb(f"{name}{m}", shape, dt, scope) for m in range(n)]

        ident = sb("ident", [P, P])
        earlier = sb("earlier", [P, P])
        trash = sb("trash", [P, G2])
        src_i = sb("src_i", [P, NG, J], i32)
        dst_i = sb("dst_i", [P, NG, J], i32)
        src_k = sb("src_k", [P, NG, J])
        dst_k = sb("dst_k", [P, NG, J])
        norm = ring("norm", 2, [P, NG, J])
        w1 = sb("w1", [D, D])
        w2 = sb("w2", [D, D])
        wlT = sb("wlT", [D, D])
        blB = sb("blB", [P, D])
        gain = sb("gain", [P, CN + J])
        sign = sb("sign", [P, 2])
        lneps = sb("lneps", [P, 1])
        cols = sb("cols", [P, 7])
        bn_s = sb("bn_s", [P, 2])
        bn_t = sb("bn_t", [P, 2])
        stat = sb("stat", [P, 2 * (NB - 1) + C, 6])
        big = sb("big", [P, max(NG * J * D + 3 * HALVES * QW, NKEPT * BN)])
        spare = big[:, NG * J * D:]
        msgs = big[:, 0:NG * J * D].rearrange("p (g f) -> p g f", g=NG)
        ykept = big[:, 0:NKEPT * BN].rearrange("p (n f) -> p n f", n=NKEPT)
        psum = [ctx.enter_context(nc.psum_tensor(f"psum{n}", [P, 2 * BANK], f32)) for n in range(4)]
        pool_go = sem("pool_go"); dve_go = sem("dve_go")

        with ExitStack() as edge_scope:
            WeB = sb("WeB", [P, J * D], f32, edge_scope)
            beB = sb("beB", [1, J * D], f32, edge_scope)
            ones = sb("ones", [1, P], f32, edge_scope)

            RN = 4
            EARLY_BIG = 2
            wide = CN * D
            assert spare.shape[1] >= 3 * wide
            xb = [t.rearrange("p (c d) -> p c d", c=CN) for t in
                  [t[:, :] for t in ring("n_x", RN - 1, [P, wide], f32, edge_scope)] + [spare[:, 2 * wide:3 * wide]]]
            n_x_loaded = [sems(f"n_x_loaded{h}_", RN) for h in range(2)]

            def big_rows(t, k, lo=0):
                base = N - P * CN if isinstance(k, int) and k == NBIG - 1 else P * CN * k
                return t[bass.ds(base + lo * CN, (P - lo) * CN), :].rearrange("(p c) d -> p (c d)", c=CN)

            def load_big(sp, i, u, h):
                part = slice(h * wide // 2, (h + 1) * wide // 2)
                sp.dma_start(xb[u].rearrange("p c d -> p (c d)")[:, part], big_rows(x, RN * i + u)[:, part]).then_inc(n_x_loaded[h][u], 16)

            params = sem("params"); indices = sem("indices"); cleared = sem("cleared"); const = sem("const")
            rows_f = sem("rows_f"); turned = sem("turned"); keys = sem("keys"); placed = sem("placed")
            sized = sem("sized"); emptied = sem("emptied"); wl_turned = sem("wl_turned")
            N_PARAMS = 2 * J + 4 + 1 + 7
            TA = min(P, NTILE); TB = NTILE - TA
            with ExitStack() as scope:
                wl = sb("wl", [D, D], f32, scope)
                w1_raw = sb("w1_raw", [D, D], f32, scope)
                epst = sb("epst", [P, 1], f32, scope)
                eps1 = sb("eps1", [P, 2], f32, scope)
                unit = sb("unit", [P, CN], f32, scope)
                trash_i = sb("trash_i", [P, G2], i32, scope)
                zeros = sb("zeros", [P, (ROWS - N) // P * D], f32, scope)
                idx_i = [ring(f"idx_i{n}", 2, [P, P], i32, scope) for n in range(2)]
                idx_f = [ring(f"idx_f{n}", 2, [P, P], f32, scope) for n in range(2)]

                with nc.Block() as block:
                    @block.sync
                    def _(sp):
                        sp.wait_ge(cleared, 3)
                        for n, edges in enumerate((src, dst)):
                            a, b = idx_i[n]
                            sp.dma_start(a[:, :], edges[0:TA * P].rearrange("(t e) -> t e", e=P)).then_inc(indices, 16)
                            sp.dma_start(b[0:TFULL - TA, :], edges[TA * P:TFULL * P].rearrange("(t e) -> t e", e=P)).then_inc(indices, 16)
                            sp.dma_start(b[TFULL - TA:TFULL - TA + 1, 0:TREST],
                                         edges[TFULL * P:E].rearrange("(t e) -> t e", t=1)).then_inc(indices, 16)
                        for j in range(J):
                            sp.dma_start(WeB[DE * j:DE * (j + 1), D * j:D * (j + 1)], We[:, :]).then_inc(params, 16)
                            sp.dma_start(beB[0:1, D * j:D * (j + 1)], be.rearrange("(a d) -> a d", a=1)).then_inc(params, 16)
                        sp.wait_ge(const, 9)
                        for t in (table, out):
                            sp.dma_start(t[N:ROWS, :].rearrange("(p r) d -> p (r d)", p=P), zeros[:, :]).then_inc(emptied, 16)
                        for u in range(EARLY_BIG):
                            for h in range(2):
                                load_big(sp, 0, u, h)
                        sp.wait_ge(params, 16 * N_PARAMS)
                        sp.wait_ge(emptied, 32)

                    @block.scalar
                    def _(act):
                        act.dma_start(epst[:, :], epsilon.rearrange("(a d) -> a d", a=1).broadcast_to((P, 1))).then_inc(params, 16)
                        for w, t in ((W1, w1_raw), (W2, w2), (Wl, wl)):
                            act.dma_start(t[:, :], w[:, :]).then_inc(params, 16)
                        act.dma_start(blB[:, :], bl.rearrange("(a d) -> a d", a=1).broadcast_to((P, D))).then_inc(params, 16)
                        for n, v in enumerate((b1, g1, beta1, b2, g2, beta2, bl)):
                            act.dma_start(cols[:, n:n + 1], v.rearrange("(p a) -> p a", a=1)).then_inc(params, 16)

                    @block.gpsimd
                    def _(pool):
                        pool.memset(idx_i[0][1][:, :], 0).then_inc(cleared, 1)
                        pool.memset(idx_i[1][1][:, :], 0).then_inc(cleared, 1)
                        pool.memset(WeB[:, :], 0.0).then_inc(cleared, 1)
                        pool.memset(ident[:, :], 0.0).then_inc(const, 1)
                        pool.memset(earlier[:, :], 1.0).then_inc(const, 1)
                        pool.memset(ones[:, :], 1.0).then_inc(const, 1)
                        pool.memset(zeros[:, :], 0.0).then_inc(const, 1)
                        pool.memset(lneps[:, :], EPS).then_inc(const, 1)
                        pool.iota(trash_i[:, :], pattern=[[P, G2]], base=N, channel_multiplier=1).then_inc(const, 1)
                        pool.wait_ge(const, 6)
                        pool.affine_select(out=ident[:, :], in_=ident[:, :], compare_op=ALU.not_equal, fill=1.0,
                                           base=0, pattern=[[-1, P]], channel_multiplier=1).then_inc(const, 1)
                        pool.affine_select(out=earlier[:, :], in_=earlier[:, :], compare_op=ALU.is_gt,
                                           fill=0.0, base=0, pattern=[[-1, P]], channel_multiplier=1).then_inc(const, 1)
                        pool.tensor_copy(trash[:, :], trash_i[:, :]).then_inc(const, 1)
                        pool.wait_ge(turned, 2)
                        for t in (src_k, dst_k):
                            pool.affine_select(out=t[:, GFULL:NG, :], in_=t[:, GFULL:NG, :], compare_op=ALU.is_gt,
                                               fill=float(PAD), base=E - GFULL * GE,
                                               pattern=[[-GE, NG - GFULL], [-P, J]], channel_multiplier=-1).then_inc(keys, 1)

                    @block.vector
                    def _(dve):
                        dve.wait_ge(indices, 16 * 6)
                        for n in range(2):
                            for h in range(2):
                                dve.tensor_copy(idx_f[n][h][:, :], idx_i[n][h][:, :]).then_inc(rows_f, 1)
                        dve.wait_ge(keys, 4)
                        for n, (k, i) in enumerate(((src_k, src_i), (dst_k, dst_i))):
                            dve.tensor_copy(flat(i), psum[n][:, 0:NTILE]).then_inc(placed, 1)
                            dve.tensor_copy(flat(k), psum[n][:, 0:NTILE]).then_inc(turned, 1)
                        dve.wait_ge(params, 16 * N_PARAMS)
                        dve.memset(unit[:, :], 1.0).then_inc(sized, 1)
                        dve.memset(sign[:, 1:2], 1.0).then_inc(sized, 1)
                        dve.memset(gain[:, CN:CN + J], 1.0).then_inc(sized, 1)
                        dve.tensor_scalar(eps1[:, 0:1], epst[:, :], 1.0, None, ALU.add).then_inc(sized, 1)
                        dve.wait_ge(sized, 4)
                        dve.tensor_scalar(eps1[:, 1:2], eps1[:, 0:1], 0.0, None, ALU.is_lt).then_inc(sized, 1)
                        dve.wait_ge(sized, 5)
                        dve.tensor_scalar(sign[:, 0:1], eps1[:, 1:2], -2.0, 1.0, ALU.mult, ALU.add).then_inc(sized, 1)
                        dve.wait_ge(sized, 6)
                        dve.tensor_scalar(gain[:, 0:CN], unit[:, :], eps1[:, 0:1], sign[:, 0:1], ALU.mult, ALU.mult).then_inc(sized, 1)
                        dve.tensor_scalar(w1[:, :], w1_raw[:, :], sign[:, 0:1], None, ALU.mult).then_inc(sized, 1)
                        dve.wait_ge(wl_turned, 1)
                        dve.tensor_copy(wlT[:, :], psum[2][:, 0:D]).then_inc(placed, 1)

                    @block.tensor
                    def _(pe):
                        pe.wait_ge(const, 9)
                        pe.wait_ge(rows_f, 4)
                        for n in range(2):
                            for h, t in enumerate((TA, TB)):
                                nc.tensor.transpose(psum[n][:, h * P:h * P + t], idx_f[n][h][0:t, :], ident[0:t, 0:t]).then_inc(keys, 1)
                        pe.wait_ge(params, 16 * N_PARAMS)
                        nc.tensor.transpose(psum[2][:, 0:D], wl[:, :], ident[:, :]).then_inc(wl_turned, 1)

            COLS = CN + J
            n_stats_taken = sem("n_stats_taken"); n_squares_ready = sem("n_squares_ready")
            n_apart_ready = sem("n_apart_ready"); n_means_ready = sem("n_means_ready")
            n_var_ready = sem("n_var_ready"); n_root_ready = sem("n_root_ready")
            n_inverse_ready = sem("n_inverse_ready")
            n_scale_ready = sem("n_scale_ready"); n_shift_ready = sem("n_shift_ready")
            n_half_normed = sem("n_half_normed"); n_stored = sems("n_stored", RN)
            g_attr_loaded = sems("g_attr_loaded", RN); g_index_copied = sem("g_index_copied")
            g_x_gathered = sems("g_x_gathered", RN); g_normed = sem("g_normed")
            g_message_made = sem("g_message_made")
            g_attr_turned = sem("g_attr_turned"); g_attr_copied = sem("g_attr_copied")
            g_product_ready = sem("g_product_ready"); g_features_ready = sem("g_features_ready")
            with ExitStack() as scope:
                hb = [spare[:, v * wide:(v + 1) * wide].rearrange("p (c d) -> p c d", c=CN) for v in range(2)]
                st = ring("n_st_", RN, [P, COLS, 6], f32, scope)
                means = ring("n_means", RN, [P, COLS], f32, scope); apart = sb("n_apart", [P, COLS], f32, scope)
                within = sb("n_within", [P, COLS], f32, scope); between = sb("n_between", [P, COLS], f32, scope)
                var = ring("n_var", RN, [P, COLS], f32, scope); sd = ring("n_sd_", RN, [P, COLS], f32, scope)
                iv = ring("n_iv_", RN, [P, COLS], f32, scope)
                rs = ring("n_rs_", RN, [P, COLS], f32, scope); nm = ring("n_nm_", RN, [P, COLS], f32, scope)
                gi = ring("g_i", RN, [P, J], i32, scope); xs = ring("g_x", RN, [P, J, D], f32, scope)
                hs = sb("g_hs", [P, J, D], f32, scope)
                ea = ring("g_ea_", RN, [P, J, DE], f32, scope); eaT = ring("g_eaT", RN, [J * DE, P], f32, scope)
                ef = ring("g_ef_", 2, [P, J, D], f32, scope)
                eaT_p = [psum[v][:, 0:P] for v in range(RN)]
                ef_p = [psum[v][:, BANK:2 * BANK] for v in range(RN)]

                def has_block(k):
                    return inside(k, NBIG)

                def statistics_before(k):
                    return COLS * k

                def from_col(k):
                    return 0 if has_block(k) else CN

                with nc.Block() as block:
                    @block.sync
                    def _(sp):
                        def load(i, u):
                            k = RN * i + u
                            if has_block(k) and not (isinstance(k, int) and k < EARLY_BIG):
                                if isinstance(k, int) and k == EARLY_BIG:
                                    sp.wait_ge(g_x_gathered[0], 16 * J)
                                for h in range(2):
                                    wait(sp, n_half_normed, 2 * (k - RN) + h + 1)
                                    load_big(sp, i, u, h)
                            edge_features(i, u)
                            if inside(k - RN, NBIG):
                                store(i - 1, u)

                        def edge_features(i, u):
                            g = RN * i + u
                            if isinstance(g, int) and g > GFULL:
                                return
                            wait(sp, g_attr_turned, g - RN + 1)
                            last = isinstance(g, int) and g == GFULL
                            n = TFULL - GFULL * J if last else J
                            sp.dma_start(ea[u][:, 0:n, :], edge_attr[bass.ds(GE * g, n * P), :].rearrange(
                                "(j p) d -> p j d", p=P)).then_inc(g_attr_loaded[u], 16)
                            if last:
                                sp.dma_start(ea[u][0:TREST, n, :], edge_attr[TFULL * P:E, :]).then_inc(g_attr_loaded[u], 16)

                        def store(i, u):
                            k = RN * i + u
                            wait(sp, n_half_normed, 2 * (k + 1))
                            lo = SEEN_BIG if isinstance(k, int) and k == NBIG - 1 else 0
                            sp.dma_start(big_rows(table, k, lo), hb[u % 2][lo:P].rearrange("p c d -> p (c d)")).then_inc(n_stored[u], 16)
                        steps(sp, NG, RN, load, RN)
                        for k in range(NG - RN, NBIG):
                            store(k // RN, k % RN)
                        for u in range(RN):
                            sp.wait_ge(n_stored[u], 16 * ((NBIG - u + RN - 1) // RN))

                    @block.gpsimd
                    def _(pool):
                        def gather(i, u):
                            g = RN * i + u
                            wait(pool, g_normed, g - RN + 1)
                            pool.sem_inc(pool_go, 1)
                            pool.tensor_copy(gi[u][:, :], kept(src_i, g)).then_inc(g_index_copied, 1)
                            wait(pool, g_index_copied, g + 1)
                            pool.sem_inc(pool_go, 1)
                            for j in range(J):
                                pool.indirect_dma_start(
                                    out=xs[u][:, j, :], out_offset=None, in_=x[:, :],
                                    in_offset=bass.IndirectOffsetOnAxis(ap=gi[u][:, j:j + 1], axis=0)).then_inc(g_x_gathered[u], 16)
                        steps(pool, NG, RN, gather, 2)

                    @block.vector
                    def _(dve):
                        def stats(i, u):
                            k = RN * i + u
                            wait(dve, n_shift_ready, k - RN + 1)
                            if has_block(k):
                                for c in range(CN):
                                    if c % C == 0:
                                        wait(dve, n_x_loaded[c // C][u], 16 * (i + 1))
                                    dve.bn_stats(st[u][:, c, :], xb[u][:, c, :]).then_inc(n_stats_taken, 1)
                            wait(dve, g_x_gathered[u], 16 * J * (i + 1))
                            for j in range(J):
                                dve.bn_stats(st[u][:, CN + j, :], xs[u][:, j, :]).then_inc(n_stats_taken, 1)

                        def chains(new, old):
                            if new:
                                k, u = RN * new[0] + new[1], new[1]
                                lo = from_col(k)
                                even, odd = st[u][:, lo:COLS, 0:3], st[u][:, lo:COLS, 3:6]
                                wait(dve, n_stats_taken, statistics_before(k) + COLS - lo)
                                dve.tensor_tensor(apart[:, lo:COLS], even[:, :, 1], odd[:, :, 1], ALU.subtract).then_inc(n_apart_ready, 1)
                            if old:
                                m, v = RN * old[0] + old[1], old[1]
                                at = from_col(m)
                                wait(dve, n_root_ready, m + 1)
                                dve.reciprocal(iv[v][:, at:COLS], sd[v][:, at:COLS]).then_inc(n_inverse_ready, 1)
                            if new:
                                wait(dve, n_apart_ready, k + 1)
                                dve.scalar_tensor_tensor(out=between[:, lo:COLS], in0=apart[:, lo:COLS], scalar=D / 4, in1=apart[:, lo:COLS],
                                                         op0=ALU.mult, op1=ALU.mult).then_inc(n_squares_ready, 1)
                                dve.tensor_tensor(within[:, lo:COLS], even[:, :, 2], odd[:, :, 2], ALU.add).then_inc(n_squares_ready, 1)
                            if old:
                                wait(dve, n_inverse_ready, m + 1)
                                dve.tensor_tensor(rs[v][:, at:COLS], gain[:, at:COLS], iv[v][:, at:COLS], ALU.mult).then_inc(n_scale_ready, 1)
                            if new:
                                dve.tensor_tensor(means[u][:, lo:COLS], even[:, :, 1], odd[:, :, 1], ALU.add).then_inc(n_means_ready, 1)
                                wait(dve, n_squares_ready, 2 * (k + 1))
                                dve.tensor_tensor(var[u][:, lo:COLS], between[:, lo:COLS], within[:, lo:COLS], ALU.add).then_inc(n_var_ready, 1)
                            if old:
                                wait(dve, n_scale_ready, m + 1)
                                wait(dve, n_means_ready, m + 1)
                                dve.scalar_tensor_tensor(out=nm[v][:, at:COLS], in0=means[v][:, at:COLS], scalar=-0.5, in1=rs[v][:, at:COLS],
                                                         op0=ALU.mult, op1=ALU.mult).then_inc(n_shift_ready, 1)

                        def messages(i, u):
                            g = RN * i + u
                            wait(dve, n_shift_ready, g + 1)
                            wait(dve, g_message_made, g)
                            for j in range(J):
                                m = dve.tensor_scalar(hs[:, j, :], xs[u][:, j, :], rs[u][:, CN + j:CN + j + 1], nm[u][:, CN + j:CN + j + 1],
                                                      ALU.mult, ALU.add)
                            m.then_inc(g_normed, 1)
                            wait(dve, g_normed, g + 1)
                            wait(dve, g_features_ready, g + 1)
                            dve.scalar_tensor_tensor(out=kept(msgs, g), in0=flat(hs), scalar=0.0, in1=flat(ef[u % 2]),
                                                     op0=ALU.max, op1=ALU.add).then_inc(g_message_made, 1)

                        def step(i, u):
                            k = RN * i + u
                            if inside(k + 2, NG):
                                stats(*moved(i, u, 2, RN))
                            chains(moved(i, u, 2, RN) if inside(k + 2, NG) else None,
                                   moved(i, u, 1, RN) if inside(k + 1, NG) else None)
                            messages(i, u)
                        stats(0, 0)
                        chains((0, 0), None)
                        chains(None, (0, 0))
                        stats(0, 1)
                        chains((0, 1), None)
                        steps(dve, NG, RN, step, RN)

                    @block.scalar
                    def _(act):
                        def root(i, u):
                            k = RN * i + u
                            lo = from_col(k)
                            wait(act, n_var_ready, k + 1)
                            act.activation(sd[u][:, lo:COLS], var[u][:, lo:COLS], ACT.Sqrt, bias=lneps[:, 0:1], scale=1.0 / D).then_inc(n_root_ready, 1)

                        def apply(i, u):
                            k = RN * i + u
                            wait(act, n_shift_ready, k + 1)
                            if inside(k - 2, NG):
                                before = moved(i, u, -2, RN)
                                wait(act, n_stored[before[1]], 16 * (before[0] + 1))
                            for c in range(CN):
                                a = act.activation(hb[u % 2][:, c, :], xb[u][:, c, :], ACT.Relu, bias=nm[u][:, c:c + 1],
                                                   scale=rs[u][:, c:c + 1])
                                if c % C == C - 1:
                                    a.then_inc(n_half_normed, 1)

                        def turn(i, u):
                            wait(act, g_attr_turned, RN * i + u + 1)
                            act.activation(eaT[u][:, :], eaT_p[u], ACT.Copy).then_inc(g_attr_copied, 1)

                        def features(i, u):
                            g = RN * i + u
                            wait(act, g_product_ready, g + 1)
                            wait(act, g_message_made, g - 1)
                            act.activation(flat(ef[u % 2]), ef_p[u], ACT.Relu).then_inc(g_features_ready, 1)

                        def step(i, u):
                            k = RN * i + u
                            if has_block(k):
                                apply(i, u)
                            if inside(k + 1, NG):
                                features(*moved(i, u, 1, RN))
                            if inside(k + 2, NG):
                                turn(*moved(i, u, 2, RN))
                                root(*moved(i, u, 2, RN))
                        turn(0, 0)
                        turn(0, 1)
                        root(0, 0)
                        root(0, 1)
                        features(0, 0)
                        steps(act, NG, RN, step, RN)

                    @block.tensor
                    def _(pe):
                        def features(i, u):
                            g = RN * i + u
                            if not (isinstance(g, int) and g > GFULL):
                                extra = 16 if isinstance(g, int) and g == GFULL else 0
                                wait(pe, g_attr_loaded[u], 16 * (i + 1) + extra)
                            wait(pe, g_attr_copied, g - RN + 1)
                            nc.tensor.transpose(eaT_p[u], flat(ea[u]), ident[:, :]).then_inc(g_attr_turned, 1)
                            wait(pe, g_features_ready, g - RN + 1)
                            nc.tensor.matmul(ef_p[u], ones[0:1, :], beB[0:1, :], start=True, stop=False)
                            wait(pe, g_attr_copied, g + 1)
                            nc.tensor.matmul(ef_p[u], eaT[u][:, :], WeB[:, :], start=False, stop=True).then_inc(g_product_ready, 1)
                        steps(pe, NG, RN, features, 2)

        class Adding:

            def __init__(self, scope, name, target, ends, keys_f, layer, G, same, kT, tot_p):
                self.target, self.ends, self.keys_f, self.layer, self.G = target, ends, keys_f, layer, G
                self.same, self.kT, self.tot_p = same, kT, tot_p
                self.groups = NTILE // G
                self.last = E // (P * G)
                assert self.groups * G == NTILE and self.last == self.groups - 1
                self.keys_loaded = sems(name + "_keys_loaded", 2); self.compared = sem(name + "_compared")
                self.tiles_counted = sem(name + "_tiles_counted")
                self.diagonal_counted = sem(name + "_diagonal_counted")
                self.gap_ready = sem(name + "_gap_ready"); self.counts_added = sem(name + "_counts_added")
                self.hop_ready = sem(name + "_hop_ready"); self.dest_ready = sem(name + "_dest_ready")
                self.padded = sem(name + "_padded"); self.summed = sem(name + "_summed")
                self.sums_copied = sem(name + "_sums_copied"); self.landed = sems(name + "_landed", 2)
                self.junk = sb(name + "junk", [P, G, P], f32, scope)
                self.junk_a = ring(name + "junk_a", 2, [P, (G - 1) * P], f32, scope)
                self.count = ring(name + "count", 2, [P, G], f32, scope)
                self.diag = ring(name + "diag", 2, [P, G], f32, scope)
                self.both = sb(name + "both", [P, G], f32, scope); self.gap = sb(name + "gap", [P, G], f32, scope)
                self.hop = sb(name + "hop", [P, G], f32, scope); self.dest = ring(name + "dest", 2, [P, G], i32, scope)
                self.pay = ring(name + "pay", 2, [P, G, D], f32, scope)

            def keys(self, k):
                return flat(self.keys_f)[:, bass.ds(k * self.G, self.G)]

            def pairs(self, u, j, lo, hi):
                first = j * (j + 1) // 2
                return self.same[u][:, (first + lo) * P:(first + hi) * P]

            def load(self, sp, i, u):
                k = 2 * i + u
                G = self.G
                n = E - self.last * G * P if isinstance(k, int) and k == self.last else G * P
                wait(sp, self.compared, G * (k - 1))
                sp.dma_start(self.kT[u][:, 0:n], self.ends[bass.ds(G * P * k, n)].rearrange(
                    "(a e) -> a e", a=1).broadcast_to((P, n))).then_inc(self.keys_loaded[u], 16)

            def compare(self, dve, i, u):
                k = 2 * i + u
                G = self.G
                if isinstance(k, int) and k == self.last:
                    dve.memset(self.kT[u][:, E - k * G * P:G * P], PAD).then_inc(self.padded, 1)
                    dve.wait_ge(self.padded, 1)
                wait(dve, self.keys_loaded[u], 16 * (i + 1))
                wait(dve, self.summed, k - 1)
                wait(dve, self.tiles_counted, (G - 1) * (k - 1))
                for j in range(G):
                    dve.tensor_scalar(self.pairs(u, j, 0, j + 1), self.kT[u][:, 0:(j + 1) * P],
                                      flat(self.keys_f)[:, bass.ds(k * G + j, 1)],
                                      sign[:, self.layer:self.layer + 1], ALU.is_equal, ALU.mult).then_inc(self.compared, 1)
                for j in range(G):
                    wait(dve, self.compared, G * k + j + 1)
                    dve.tensor_tensor_reduce(out=self.junk[:, j, :], in0=self.pairs(u, j, j, j + 1), in1=earlier[:, :],
                                             scale=1.0, scalar=0.0, op0=ALU.mult, op1=ALU.add,
                                             accum_out=self.diag[u][:, j:j + 1]).then_inc(self.diagonal_counted, 1)

            def place(self, dve, i, u):
                k = 2 * i + u
                G = self.G
                dve.tensor_tensor(self.gap[:, :], trash[:, 0:G], self.keys(k), ALU.subtract).then_inc(self.gap_ready, 1)
                wait(dve, self.diagonal_counted, G * (k + 1))
                wait(dve, self.tiles_counted, (G - 1) * (k + 1))
                dve.tensor_tensor(self.both[:, 1:G], self.diag[u][:, 1:G], self.count[u][:, 1:G], ALU.add).then_inc(self.counts_added, 1)
                dve.tensor_copy(self.both[:, 0:1], self.diag[u][:, 0:1]).then_inc(self.counts_added, 1)
                wait(dve, self.gap_ready, k + 1)
                wait(dve, self.counts_added, 2 * (k + 1))
                dve.scalar_tensor_tensor(out=self.hop[:, :], in0=self.both[:, :], scalar=0.0, in1=self.gap[:, :],
                                         op0=ALU.not_equal, op1=ALU.mult).then_inc(self.hop_ready, 1)
                wait(dve, self.hop_ready, k + 1)
                wait(dve, self.landed[u], 16 * G * i)
                dve.tensor_tensor(self.dest[u][:, :], self.hop[:, :], self.keys(k), ALU.add).then_inc(self.dest_ready, 1)

            def earlier_tiles(self, act, i, u):
                k = 2 * i + u
                G = self.G
                wait(act, self.counts_added, 2 * (k - 1))
                for j in range(1, G):
                    wait(act, self.compared, G * k + j + 1)
                    wait(act, self.tiles_counted, (G - 1) * k + j - 2)
                    act.activation(self.junk_a[j % 2][:, 0:j * P], self.pairs(u, j, 0, j), ACT.Copy,
                                   accum_out=self.count[u][:, j:j + 1]).then_inc(self.tiles_counted, 1)

            def sums(self, pe, i, u, banks=None):
                k = 2 * i + u
                G = self.G
                tot = self.tot_p[u] if banks is None else banks
                wait(pe, self.compared, G * (k + 1))
                wait(pe, self.sums_copied, k - 1 if banks is None else k)
                rows = flat(msgs)[:, bass.ds(k * G * D, G * D)]
                for o in range(G):
                    for j in range(o, G):
                        m = nc.tensor.matmul(tot[:, o * D:(o + 1) * D], self.pairs(u, j, o, o + 1),
                                             rows[:, j * D:(j + 1) * D], start=(j == o), stop=(j == G - 1))
                m.then_inc(self.summed, 1)

            def keep(self, act, i, u, banks=None):
                tot = self.tot_p[u] if banks is None else banks
                wait(act, self.summed, 2 * i + u + 1)
                wait(act, self.landed[u], 16 * self.G * i)
                act.activation(flat(self.pay[u]), tot[:, 0:self.G * D], ACT.Copy).then_inc(self.sums_copied, 1)

            def add(self, pool, i, u):
                k = 2 * i + u
                wait(pool, self.sums_copied, k + 1)
                wait(pool, self.dest_ready, k + 1)
                wait(pool, self.landed[1 - u], 16 * self.G * (i + u))
                pool.sem_inc(pool_go, 1)
                for j in range(self.G):
                    pool.indirect_dma_start(
                        out=self.target[:, :], out_offset=bass.IndirectOffsetOnAxis(ap=self.dest[u][:, j:j + 1], axis=0),
                        in_=self.pay[u][:, j, :], in_offset=None, compute_op=ALU.add).then_inc(self.landed[u], 16)

            def all_landed(self, pool):
                for u in range(2):
                    pool.wait_ge(self.landed[u], 16 * self.G * ((self.groups - u + 1) // 2))

        one_hots_ready = sem("one_hots_ready"); one_hots_used = sem("one_hots_used")
        degree_ready = sem("degree_ready"); root_ready = sem("root_ready")
        inv_root_ready = sem("inv_root_ready"); iota_ready = sem("iota_ready"); key_parts_ready = sem("key_parts_ready")
        with ExitStack() as scope:
            first = Adding(scope, "s", table, dst, dst_k, 0, G1, ring("s_same", 2, [P, G1 * (G1 + 1) // 2 * P], f32, scope),
                           ring("s_keys", 2, [P, G1 * P], i32, scope), [psum[1], psum[2]])
            RW = HALVES * P
            iota_i = sb("iota_i", [P, QW], i32, scope); iota_f = sb("iota_f", [P, QW], f16, scope)
            key_i = sb("key_i", [P, NTILE], i32, scope); half_i = ring("half_i", 2, [P, NTILE], i32, scope)
            half_f = ring("half_f", 2, [P, NTILE], f32, scope)
            hot_r = ring("hot_r", G1, [P, RW], f16, scope); hot_c = ring("hot_c", G1, [P, QW], f16, scope)
            deg, root, inv = (spare[:, n * HALVES * QW:(n + 1) * HALVES * QW] for n in range(3))
            assert HALVES == 2 and QW == BANK
            deg_p = psum[0][:, :]

            with nc.Block() as block:
                @block.sync
                def _(sp):
                    steps(sp, first.groups, 2, lambda i, u: first.load(sp, i, u), 1)
                    sp.wait_ge(inv_root_ready, 2)
                    for h in range(HALVES):
                        sp.dma_start(dis_tab[h * P * QW:(h + 1) * P * QW, :].rearrange("(p q) a -> p (q a)", q=QW),
                                     inv[:, h * QW:(h + 1) * QW]).then_inc(inv_root_ready, 16)
                    sp.wait_ge(inv_root_ready, 2 + 16 * HALVES)

                @block.gpsimd
                def _(pool):
                    pool.iota(iota_i[:, :], pattern=[[1, QW]], base=0, channel_multiplier=0).then_inc(iota_ready, 1)
                    pool.wait_ge(iota_ready, 1)
                    pool.tensor_copy(iota_f[:, :], iota_i[:, :]).then_inc(iota_ready, 1)
                    steps(pool, first.groups, 2, lambda i, u: first.add(pool, i, u), 1)
                    first.all_landed(pool)

                @block.vector
                def _(dve):
                    def one_hots(i, u):
                        k = 2 * i + u
                        wait(dve, one_hots_used, G1 * k)
                        for j in range(G1):
                            dve.tensor_scalar(hot_r[j][:, :], iota_f[:, 0:RW], half_f[0][:, bass.ds(G1 * k + j, 1)], None, ALU.is_equal).then_inc(one_hots_ready, 1)
                            dve.tensor_scalar(hot_c[j][:, :], iota_f[:, :], half_f[1][:, bass.ds(G1 * k + j, 1)], None, ALU.is_equal).then_inc(one_hots_ready, 1)

                    def split_keys():
                        dve.tensor_copy(key_i[:, :], flat(src_k)).then_inc(key_parts_ready, 1)
                        dve.wait_ge(key_parts_ready, 1)
                        dve.tensor_scalar(half_i[0][:, :], key_i[:, :], QB, None, ALU.logical_shift_right).then_inc(key_parts_ready, 1)
                        dve.tensor_scalar(half_i[1][:, :], key_i[:, :], QW - 1, None, ALU.bitwise_and).then_inc(key_parts_ready, 1)
                        dve.wait_ge(key_parts_ready, 3)
                        dve.tensor_copy(half_f[0][:, :], half_i[0][:, :]).then_inc(key_parts_ready, 1)
                        dve.tensor_copy(half_f[1][:, :], half_i[1][:, :]).then_inc(key_parts_ready, 1)
                        dve.wait_ge(key_parts_ready, 5)
                        dve.wait_ge(iota_ready, 2)

                    def step(i, u):
                        first.compare(dve, i, u)
                        if isinstance(i, int) and i == 0 and u == 0:
                            split_keys()
                        one_hots(i, u)
                        first.place(dve, i, u)
                    steps(dve, first.groups, 2, step, 1)
                    dve.wait_ge(one_hots_used, NTILE)
                    dve.tensor_scalar(deg[:, :], deg_p, 1.0, None, ALU.max).then_inc(degree_ready, 1)
                    dve.wait_ge(root_ready, 1)
                    dve.reciprocal(inv[:, :], root[:, :]).then_inc(inv_root_ready, 1)
                    dve.wait_ge(inv_root_ready, 1)
                    dve.scalar_tensor_tensor(out=inv[:, :], in0=deg_p, scalar=0.0, in1=inv[:, :],
                                             op0=ALU.is_gt, op1=ALU.mult).then_inc(inv_root_ready, 1)

                @block.tensor
                def _(pe):
                    def step(i, u):
                        k = 2 * i + u
                        first.sums(pe, i, u)
                        for j in range(G1):
                            begin = isinstance(k, int) and k == 0 and j == 0
                            final = isinstance(k, int) and k == first.groups - 1 and j == G1 - 1
                            wait(pe, one_hots_ready, 2 * (G1 * k + j + 1))
                            for h in range(HALVES):
                                m = nc.tensor.matmul(psum[0][:, h * QW:(h + 1) * QW], hot_r[j][:, h * P:(h + 1) * P],
                                                     hot_c[j][:, :], start=begin, stop=final)
                            m.then_inc(one_hots_used, 1)
                    steps(pe, first.groups, 2, step, 1)

                @block.scalar
                def _(act):
                    def step(i, u):
                        if inside(2 * i + u + 1, first.groups):
                            first.earlier_tiles(act, *moved(i, u, 1, 2))
                        first.keep(act, i, u)
                    first.earlier_tiles(act, 0, 0)
                    steps(act, first.groups, 2, step, 2)
                    act.wait_ge(degree_ready, 1)
                    act.activation(root[:, :], deg[:, :], ACT.Sqrt).then_inc(root_ready, 1)

        def stat_slices(k, y):
            if tail(k):
                return [(2 * (NB - 1) + c, y[:, c * P + SEEN:(c + 1) * P]) for c in range(C)]
            return [(2 * k + h, y[:, h * BANK:(h + 1) * BANK]) for h in range(2)]

        def take_stats(dve, k, y):
            for n, part in stat_slices(k, y):
                m = dve.bn_stats(kept(stat, n), part)
            return m

        bn_chain = sem("bn_chain"); bn_root = sem("bn_root")

        def batch_norm(dve, n, mvt, tmp):
            b, g, beta = (cols[:, 3 * n + m:3 * n + m + 1] for m in range(3))

            def link(ins, m):
                ins.then_inc(bn_chain, 1)
                dve.wait_ge(bn_chain, 6 * n + m)
            link(dve.bn_aggr(mvt[:, 0:2], flat(stat)), 1)
            dve.wait_ge(bn_root, n + 1)
            link(dve.reciprocal(tmp[:, 1:2], tmp[:, 0:1]), 2)
            link(dve.tensor_tensor(bn_s[:, n:n + 1], g, tmp[:, 1:2], ALU.mult), 3)
            link(dve.tensor_tensor(tmp[:, 2:3], mvt[:, 0:1], b, ALU.add), 4)
            link(dve.tensor_tensor(tmp[:, 3:4], b, tmp[:, 2:3], ALU.subtract), 5)
            link(dve.scalar_tensor_tensor(out=bn_t[:, n:n + 1], in0=tmp[:, 3:4], scalar=bn_s[:, n:n + 1], in1=beta,
                                          op0=ALU.mult, op1=ALU.add), 6)

        def bn_square_root(act, n, mvt, tmp):
            act.wait_ge(bn_chain, 6 * n + 1)
            act.activation(tmp[:, 0:1], mvt[:, 1:2], ACT.Sqrt, bias=lneps[:, 0:1]).then_inc(bn_root, 1)

        def kept_y(i, u):
            return kept(ykept, len(KEPT) * i + KEPT.index(u))

        def in_sbuf(u):
            return u in KEPT

        d_index_copied = sem("d_index_copied"); d_gathered = sems("d_gathered", 2); d_kept = sem("d_kept")

        def gather_degrees(pool, n, ends, start, end, gi, gv):
            def gather(i, v):
                k = start + 2 * i + v
                wait(pool, d_kept, NG * n + k - 1)
                pool.sem_inc(pool_go, 1)
                pool.tensor_copy(gi[v][:, :], kept(ends, k)).then_inc(d_index_copied, 1)
                wait(pool, d_index_copied, NG * n + k + 1)
                pool.sem_inc(pool_go, 1)
                for j in range(J):
                    pool.indirect_dma_start(
                        out=gv[v][:, j:j + 1], out_offset=None, in_=dis_tab[:, :],
                        in_offset=bass.IndirectOffsetOnAxis(ap=gi[v][:, j:j + 1], axis=0)).then_inc(d_gathered[v], 16)

            def keep(i, v):
                k = start + 2 * i + v
                wait(pool, d_gathered[v], 16 * J * ((NG * n + start) // 2 + i + 1))
                pool.sem_inc(pool_go, 1)
                pool.tensor_copy(kept(norm[n], k), gv[v][:, :]).then_inc(d_kept, 1)

            def step(i, v):
                if inside(2 * i + v + 1, end - start):
                    gather(*moved(i, v, 1, 2))
                keep(i, v)
            gather(0, 0)
            steps(pool, end - start, 2, step, 1)

        pass_scope = ExitStack()
        rows = ring("rows", B, [P, C, D], f32, pass_scope)
        ys = ring("ys", len(SPILT), [P, BN], f32, pass_scope)
        feats = ring("feats", 2, [P, BN], f32, pass_scope)
        p2_loaded = spilt_sems("p2_loaded"); p3_y_loaded = spilt_sems("p3_y_loaded")
        p3_x_loaded = sems("p3_x_loaded", B)

        def load_y1(sp, sem, i, u):
            sp.dma_start(ys[SPILT.index(u)][:, :], spilled(y1_s, B * i + u)).then_inc(sem[u], 16)

        def load_x(sp, i, u):
            sp.dma_start(flat(rows[u]), node_rows(x, B * i + u)).then_inc(p3_x_loaded[u], 16)

        def in_first_turn(i):
            return isinstance(i, int) and i == 0

        p1_loaded = sems("p1_loaded", B); p1_turned = sem("p1_turned"); p1_turned_copied = sem("p1_turned_copied")
        p1_product_ready = sem("p1_product_ready"); p1_stats_taken = sem("p1_stats_taken")
        p1_y_copied = sem("p1_y_copied"); p1_stored = spilt_sems("p1_stored")
        with ExitStack() as scope:
            mvt = sb("mvt1", [P, 2], f32, scope); tmp = sb("tmp1", [P, 4], f32, scope)
            gi = ring("p1_gi", 2, [P, J], i32, scope); gv = ring("p1_gv", 2, [P, J], f32, scope)

            with nc.Block() as block:
                @block.sync
                def _(sp):
                    def load(i, u):
                        k = B * i + u
                        wait(sp, p1_turned, k - B + 1)
                        sp.dma_start(flat(rows[u]), node_rows(table, k)).then_inc(p1_loaded[u], 16)
                        if inside(k - LAG, NB):
                            store(*moved(i, u, -LAG, B))

                    def store(i, u):
                        k = B * i + u
                        if in_sbuf(u):
                            return
                        wait(sp, p1_y_copied, k + 1)
                        sp.dma_start(spilled(y1_s, k), ys[SPILT.index(u)][:, :]).then_inc(p1_stored[u], 16)
                    steps(sp, NB, B, load, 2)
                    for k in range(NB - LAG, NB):
                        store(k // B, k % B)
                    for u in SPILT:
                        sp.wait_ge(p1_stored[u], 16 * ((NB - u + B - 1) // B))
                        load_y1(sp, p2_loaded, 0, u)

                @block.gpsimd
                def _(pool):
                    gather_degrees(pool, 0, src_i, 0, NG, gi, gv)

                @block.tensor
                def _(pe):
                    def turn(i, u):
                        k = B * i + u
                        wait(pe, p1_loaded[u], 16 * (i + 1))
                        wait(pe, p1_turned_copied, k - 1)
                        for c in range(C):
                            m = nc.tensor.transpose(psum[u % 2][:, c * P:(c + 1) * P], rows[u][:, c, :], ident[:, :])
                        m.then_inc(p1_turned, 1)

                    def step(i, u):
                        k = B * i + u
                        if inside(k + 1, NB):
                            turn(*moved(i, u, 1, B))
                        wait(pe, p1_turned_copied, k + 1)
                        wait(pe, p1_y_copied, k - 1)
                        for h in range(2):
                            m = nc.tensor.matmul(psum[2 + u % 2][:, h * BANK:(h + 1) * BANK], w1[:, :],
                                                 feats[u % 2][:, h * BANK:(h + 1) * BANK], start=True, stop=True)
                        m.then_inc(p1_product_ready, 1)
                    turn(0, 0)
                    steps(pe, NB, B, step, 2)

                @block.scalar
                def _(act):
                    def step(i, u):
                        k = B * i + u
                        wait(act, p1_turned, k + 1)
                        wait(act, p1_product_ready, k - 1)
                        act.activation(feats[u % 2][:, :], psum[u % 2][:, :], ACT.Copy).then_inc(p1_turned_copied, 1)
                    steps(act, NB, B, step, 2)
                    bn_square_root(act, 0, mvt, tmp)

                @block.vector
                def _(dve):
                    def step(i, u):
                        k = B * i + u
                        wait(dve, p1_product_ready, k + 1)
                        take_stats(dve, k, psum[2 + u % 2]).then_inc(p1_stats_taken, 1)
                        if in_sbuf(u):
                            y = kept_y(i, u)
                        else:
                            y = ys[SPILT.index(u)][:, :]
                            wait(dve, p1_stored[u], 16 * i)
                        dve.tensor_copy(y, psum[2 + u % 2][:, :]).then_inc(p1_y_copied, 1)
                    steps(dve, NB, B, step, 2)
                    dve.wait_ge(p1_stats_taken, NB)
                    batch_norm(dve, 0, mvt, tmp)

        p2_relu_done = sem("p2_relu_done"); p2_product_ready = sem("p2_product_ready")
        p2_stats_taken = sem("p2_stats_taken")
        with ExitStack() as scope:
            mvt = sb("mvt2", [P, 2], f32, scope); tmp = sb("tmp2", [P, 4], f32, scope)
            gi = ring("p2_gi", 2, [P, J], i32, scope); gv = ring("p2_gv", 2, [P, J], f32, scope)

            with nc.Block() as block:
                @block.sync
                def _(sp):
                    def load(i, u):
                        k = B * i + u
                        if not in_sbuf(u) and not in_first_turn(i):
                            wait(sp, p2_relu_done, k - B + 1)
                            load_y1(sp, p2_loaded, i, u)
                    for u in range(B):
                        load_x(sp, 0, u)
                    steps(sp, NB, B, load, 2)
                    sp.wait_ge(p2_relu_done, NB)
                    for u in SPILT:
                        load_y1(sp, p3_y_loaded, 0, u)

                @block.gpsimd
                def _(pool):
                    gather_degrees(pool, 1, dst_i, 0, CUT, gi, gv)

                @block.scalar
                def _(act):
                    def relu(i, u):
                        k = B * i + u
                        if in_sbuf(u):
                            y = kept_y(i, u)
                        else:
                            wait(act, p2_loaded[u], 16 * (i + 1))
                            y = ys[SPILT.index(u)][:, :]
                        wait(act, p2_product_ready, k - 1)
                        act.activation(feats[u % 2][:, :], y, ACT.Relu, bias=bn_t[:, 0:1], scale=bn_s[:, 0:1]).then_inc(p2_relu_done, 1)
                    steps(act, NB, B, relu, 2)
                    bn_square_root(act, 1, mvt, tmp)

                @block.tensor
                def _(pe):
                    def step(i, u):
                        k = B * i + u
                        wait(pe, p2_relu_done, k + 1)
                        wait(pe, p2_stats_taken, k - 2)
                        for h in range(2):
                            m = nc.tensor.matmul(psum[u % 3][:, h * BANK:(h + 1) * BANK], w2[:, :],
                                                 feats[u % 2][:, h * BANK:(h + 1) * BANK], start=True, stop=True)
                        m.then_inc(p2_product_ready, 1)
                    steps(pe, NB, B, step, 2)

                @block.vector
                def _(dve):
                    def step(i, u):
                        k = B * i + u
                        wait(dve, p2_product_ready, k + 1)
                        take_stats(dve, k, psum[u % 3]).then_inc(p2_stats_taken, 1)
                    steps(dve, NB, B, step, 2)
                    dve.wait_ge(p2_stats_taken, NB)
                    batch_norm(dve, 1, mvt, tmp)

        p3_relu1_done = sem("p3_relu1_done"); p3_product_ready = sem("p3_product_ready")
        p3_relu2_done = sem("p3_relu2_done")
        p3_bias_added = sem("p3_bias_added"); p3_turned = sem("p3_turned"); p3_x_added = sem("p3_x_added")
        p3_stored = sems("p3_stored", B)
        with ExitStack() as scope:
            zb = ring("p3_z_", 2, [P, BN], f32, scope)
            gi = ring("p3_gi", 2, [P, J], i32, scope); gv = ring("p3_gv", 2, [P, J], f32, scope)

            with nc.Block() as block:
                @block.sync
                def _(sp):
                    def load(i, u):
                        k = B * i + u
                        if not in_sbuf(u) and not in_first_turn(i):
                            wait(sp, p3_relu1_done, k - B + 1)
                            load_y1(sp, p3_y_loaded, i, u)
                        if not in_first_turn(i):
                            wait(sp, p3_stored[u], 16 * i)
                            load_x(sp, i, u)
                        if inside(k - LAG, NB):
                            store(*moved(i, u, -LAG, B))

                    def store(i, u):
                        k = B * i + u
                        wait(sp, p3_x_added, k + 1)
                        lo = SEEN if tail(k) else 0
                        sp.dma_start(node_rows(out, k, lo), flat(rows[u][lo:P])).then_inc(p3_stored[u], 16)
                    steps(sp, NB, B, load, 2)
                    for k in range(NB - LAG, NB):
                        store(k // B, k % B)
                    for u in range(B):
                        sp.wait_ge(p3_stored[u], 16 * ((NB - u + B - 1) // B))

                @block.gpsimd
                def _(pool):
                    gather_degrees(pool, 1, dst_i, CUT, NG, gi, gv)

                @block.scalar
                def _(act):
                    def relu1(i, u):
                        k = B * i + u
                        if in_sbuf(u):
                            y = kept_y(i, u)
                        else:
                            wait(act, p3_y_loaded[u], 16 * (i + 1))
                            y = ys[SPILT.index(u)][:, :]
                        wait(act, p3_product_ready, k - 1)
                        act.activation(feats[u % 2][:, :], y, ACT.Relu, bias=bn_t[:, 0:1], scale=bn_s[:, 0:1]).then_inc(p3_relu1_done, 1)

                    def step(i, u):
                        k = B * i + u
                        if inside(k + 1, NB):
                            relu1(*moved(i, u, 1, B))
                        wait(act, p3_product_ready, k + 1)
                        wait(act, p3_turned, k - 1)
                        act.activation(zb[u % 2][:, :], psum[u % 2][:, :], ACT.Relu, bias=bn_t[:, 1:2], scale=bn_s[:, 1:2]).then_inc(p3_relu2_done, 1)
                    relu1(0, 0)
                    steps(act, NB, B, step, 2)

                @block.tensor
                def _(pe):
                    def product(i, u):
                        k = B * i + u
                        wait(pe, p3_relu1_done, k + 1)
                        wait(pe, p3_relu2_done, k - 1)
                        for h in range(2):
                            m = nc.tensor.matmul(psum[u % 2][:, h * BANK:(h + 1) * BANK], w2[:, :],
                                                 feats[u % 2][:, h * BANK:(h + 1) * BANK], start=True, stop=True)
                        m.then_inc(p3_product_ready, 1)

                    def step(i, u):
                        k = B * i + u
                        if inside(k + 1, NB):
                            product(*moved(i, u, 1, B))
                        wait(pe, p3_bias_added, k + 1)
                        wait(pe, p3_x_added, k - 1)
                        for c in range(C):
                            m = nc.tensor.transpose(psum[2 + u % 2][:, c * P:(c + 1) * P], zb[u % 2][:, c * P:(c + 1) * P], ident[:, :])
                        m.then_inc(p3_turned, 1)
                    product(0, 0)
                    steps(pe, NB, B, step, 2)

                @block.vector
                def _(dve):
                    def bias(i, u):
                        k = B * i + u
                        wait(dve, p3_relu2_done, k + 1)
                        dve.tensor_scalar(zb[u % 2][:, :], zb[u % 2][:, :], cols[:, 6:7], None, ALU.add).then_inc(p3_bias_added, 1)

                    def step(i, u):
                        k = B * i + u
                        if inside(k + 1, NB):
                            bias(*moved(i, u, 1, B))
                        wait(dve, p3_turned, k + 1)
                        wait(dve, p3_x_loaded[u], 16 * (i + 1))
                        dve.tensor_tensor(flat(rows[u]), psum[2 + u % 2][:, :], flat(rows[u]), ALU.add).then_inc(p3_x_added, 1)
                    bias(0, 0)
                    steps(dve, NB, B, step, 2)

        pass_scope.close()

        m_index_copied = sem("m_index_copied"); m_gathered = sems("m_gathered", R)
        m_bias_removed = sem("m_bias_removed"); m_stats_taken = sem("m_stats_taken")
        m_var_ready = sem("m_var_ready"); m_root_ready = sem("m_root_ready")
        m_scale_ready = sem("m_scale_ready"); m_shift_ready = sem("m_shift_ready"); m_normed = sem("m_normed")
        m_turned = sem("m_turned"); m_turned_copied = sem("m_turned_copied")
        m_product_ready = sem("m_product_ready"); m_message_made = sem("m_message_made")
        m_norm_ready = sem("m_norm_ready")
        with ExitStack() as scope:
            gi = ring("m_gi_", R, [P, J], i32, scope); xs = ring("m_xs_", R, [P, J, D], f32, scope)
            x2 = ring("m_x2_", R, [P, J, D], f32, scope)
            st = ring("m_st_", R, [P, J, 6], f32, scope); mv = ring("m_mv_", R, [P, J, 2], f32, scope)
            sd = ring("m_sd_", R, [P, J], f32, scope)
            rs = ring("m_rs_", R, [P, J], f32, scope); nm = ring("m_nm_", R, [P, J], f32, scope)
            hs = ring("m_hs_", R, [P, J, D], f32, scope); hT = ring("m_hT_", R, [P, GE], f32, scope)
            hT_p = [psum[0][:, 0:BANK], psum[0][:, BANK:2 * BANK], psum[1][:, 0:BANK]]
            w_p = [psum[2][:, 0:BANK], psum[2][:, BANK:2 * BANK], psum[1][:, BANK:2 * BANK]]
            size = G2 * (G2 + 1) // 2 * P
            t_keys = [spare[:, size + v * G2 * P:size + (v + 1) * G2 * P].bitcast(i32) for v in range(2)]
            second = Adding(scope, "t", out, src, src_k, 1, G2, [spare[:, 0:size], sb("t_same", [P, size], f32, scope)],
                            t_keys, [psum[3], psum[2]])
            EARLY, LATE, LATER = R - 1, NG - 20, NG - 11
            PEEL = NG - LATE + 1

            def at(k, step):
                return isinstance(k, int) and k == step

            with nc.Block() as block:
                @block.sync
                def _(sp):
                    steps(sp, second.groups, 2, lambda i, u: second.load(sp, i, u), 1)

                @block.gpsimd
                def _(pool):
                    def gather(i, u):
                        k = R * i + u
                        wait(pool, m_index_copied, k + 1)
                        pool.sem_inc(pool_go, 1)
                        for j in range(J):
                            pool.indirect_dma_start(
                                out=xs[u][:, j, :], out_offset=None, in_=out[:, :],
                                in_offset=bass.IndirectOffsetOnAxis(ap=gi[u][:, j:j + 1], axis=0)).then_inc(m_gathered[u], 16)
                    steps(pool, NG, R, gather, 1)
                    pool.wait_ge(m_bias_removed, NG)
                    steps(pool, second.groups, 2, lambda i, u: second.add(pool, i, u), 1)
                    second.all_landed(pool)

                @block.vector
                def _(dve):
                    def indices(i, u):
                        dve.tensor_copy(gi[u][:, :], kept(dst_i, R * i + u)).then_inc(m_index_copied, 1)

                    def stats(i, u):
                        k = R * i + u
                        wait(dve, m_gathered[u], 16 * J * (i + 1))
                        wait(dve, m_normed, k - R + 1)
                        dve.tensor_tensor(x2[u][:, :, :], xs[u][:, :, :], blB[:, :].rearrange("p (a d) -> p a d", a=1).broadcast_to((P, J, D)),
                                          ALU.subtract).then_inc(m_bias_removed, 1)
                        wait(dve, m_bias_removed, k + 1)
                        if inside(k + R, NG):
                            indices(*moved(i, u, R, R))
                        for j in range(J):
                            dve.bn_stats(st[u][:, j, :], x2[u][:, j, :]).then_inc(m_stats_taken, 1)
                        wait(dve, m_stats_taken, J * (k + 1))
                        dve.sem_inc(dve_go, 1)
                        for j in range(J):
                            m = dve.bn_aggr(mv[u][:, j, :], st[u][:, j, :])
                        m.then_inc(m_var_ready, 1)

                    def invert(i, u):
                        k = R * i + u
                        wait(dve, m_root_ready, k + 1)
                        dve.reciprocal(rs[u][:, :], sd[u][:, :]).then_inc(m_scale_ready, 1)
                        wait(dve, m_scale_ready, k + 1)
                        dve.scalar_tensor_tensor(out=nm[u][:, :], in0=mv[u][:, :, 0], scalar=-1.0, in1=rs[u][:, :],
                                                 op0=ALU.mult, op1=ALU.mult).then_inc(m_shift_ready, 1)

                    def weigh(i, u):
                        k = R * i + u
                        wait(dve, m_product_ready, k + 1)
                        dve.tensor_tensor(msgs[:, bass.ds(k, 1), :].rearrange("p a (j d) -> p (a j) d", j=J),
                                          w_p[u].rearrange("p (j d) -> p j d", j=J),
                                          norm[0][:, bass.ds(k, 1), :].rearrange("p a j -> p j a").broadcast_to((P, J, D)),
                                          ALU.mult).then_inc(m_message_made, 1)

                    def step(i, u):
                        k = R * i + u
                        if inside(k + 1, NG):
                            invert(*moved(i, u, 1, R))
                        if inside(k - 1, NG):
                            weigh(*moved(i, u, -1, R))
                        if inside(k + 2, NG):
                            stats(*moved(i, u, 2, R))
                        if at(k, EARLY):
                            second.compare(dve, 0, 0)
                        if at(k, LATE):
                            second.place(dve, 0, 0)
                            second.compare(dve, 0, 1)
                        if at(k, LATER):
                            second.place(dve, 0, 1)
                            second.compare(dve, 1, 0)

                    def adding(i, u):
                        k = 2 * i + u
                        if not (isinstance(k, int) and k <= 2):
                            second.compare(dve, i, u)
                        if not (isinstance(k, int) and k < 2):
                            second.place(dve, i, u)
                    for u in range(R):
                        indices(0, u)
                    dve.tensor_tensor(norm[0][:, :, :], norm[0][:, :, :], norm[1][:, :, :], ALU.mult).then_inc(m_norm_ready, 1)
                    dve.wait_ge(m_norm_ready, 1)
                    stats(0, 0)
                    stats(0, 1)
                    invert(0, 0)
                    steps(dve, NG, R, step, PEEL)
                    weigh((NG - 1) // R, (NG - 1) % R)
                    steps(dve, second.groups, 2, adding, 1, turns=2)

                @block.scalar
                def _(act):
                    def root(i, u):
                        wait(act, m_var_ready, R * i + u + 1)
                        act.activation(sd[u][:, :], mv[u][:, :, 1], ACT.Sqrt, bias=lneps[:, 0:1]).then_inc(m_root_ready, 1)

                    def relu(i, u):
                        k = R * i + u
                        wait(act, m_shift_ready, k + 1)
                        wait(act, m_turned, k - R + 1)
                        for j in range(J):
                            a = act.activation(hs[u][:, j, :], x2[u][:, j, :], ACT.Relu, bias=nm[u][:, j:j + 1],
                                               scale=rs[u][:, j:j + 1])
                        a.then_inc(m_normed, 1)

                    def step(i, u):
                        k = R * i + u
                        wait(act, m_turned, k + 1)
                        wait(act, m_product_ready, k - R + 1)
                        act.activation(hT[u][:, :], hT_p[u], ACT.Copy).then_inc(m_turned_copied, 1)
                        if inside(k + 1, NG):
                            relu(*moved(i, u, 1, R))
                        if inside(k + 2, NG):
                            root(*moved(i, u, 2, R))
                        if at(k, EARLY):
                            second.earlier_tiles(act, 0, 0)
                        if at(k, LATE):
                            second.earlier_tiles(act, 0, 1)
                        if at(k, LATE + 3):
                            second.keep(act, 0, 0)
                        if at(k, LATER + 3):
                            second.keep(act, 0, 1, psum[3])

                    def adding(i, u):
                        if inside(2 * i + u + 1, second.groups) and not at(2 * i + u, 0):
                            second.earlier_tiles(act, *moved(i, u, 1, 2))
                        if not (isinstance(i, int) and i == 0):
                            second.keep(act, i, u)
                    root(0, 0)
                    root(0, 1)
                    relu(0, 0)
                    steps(act, NG, R, step, PEEL)
                    steps(act, second.groups, 2, adding, 2)

                @block.tensor
                def _(pe):
                    def turn(i, u):
                        k = R * i + u
                        wait(pe, m_normed, k + 1)
                        wait(pe, m_turned_copied, k - R + 1)
                        for j in range(J):
                            m = nc.tensor.transpose(hT_p[u][:, j * P:(j + 1) * P], hs[u][:, j, :], ident[:, :])
                        m.then_inc(m_turned, 1)

                    def step(i, u):
                        k = R * i + u
                        wait(pe, m_turned_copied, k + 1)
                        wait(pe, m_message_made, k - R + 1)
                        for j in range(J):
                            m = nc.tensor.matmul(w_p[u][:, j * D:(j + 1) * D], hT[u][:, j * P:(j + 1) * P], wlT[:, :], start=True, stop=True)
                        m.then_inc(m_product_ready, 1)
                        if inside(k + 1, NG):
                            turn(*moved(i, u, 1, R))
                        if at(k, LATE):
                            second.sums(pe, 0, 0)
                        if at(k, LATER):
                            second.sums(pe, 0, 1, psum[3])

                    def adding(i, u):
                        if not (isinstance(i, int) and i == 0):
                            second.sums(pe, i, u)
                    turn(0, 0)
                    steps(pe, NG, R, step, PEEL)
                    pe.wait_ge(m_message_made, NG)
                    pe.wait_ge(second.sums_copied, 2)
                    steps(pe, second.groups, 2, adding, 1)


_INS = ['x', 'src', 'dst', 'edge_attr_32', 'L0_gnn_epsilon', 'L0_gnn_We', 'L0_gnn_be', 'L0_gnn_W1', 'L0_gnn_b1',
        'L0_gnn_g1', 'L0_gnn_beta1', 'L0_gnn_W2', 'L0_gnn_b2', 'L0_gnn_g2', 'L0_gnn_beta2', 'L1_gnn_W', 'L1_gnn_b']
_TRASH = 9 * 128


def kernel(**inputs):
    import numpy as _np
    import concourse.bacc as _bacc
    from concourse import mybir as _mybir
    from concourse.bass_utils import run_bass_kernel_spmd as _run

    nc = _bacc.Bacc("TRN2", target_bir_lowering=False, num_devices=1)
    arrays, args = {}, []
    for name in _INS:
        a = _np.ascontiguousarray(inputs[name])
        arrays[f"in_{name}_dram"] = a
        args.append(nc.dram_tensor(f"in_{name}_dram", a.shape, _mybir.dt.from_np(a.dtype), kind="ExternalInput").ap())
    n, d = inputs["x"].shape
    args.append(nc.dram_tensor("out_0_dram", (n + _TRASH, d), _mybir.dt.float32, kind="ExternalOutput").ap())
    preln_gin_then_gcn(nc, *args)
    r = _run(nc, [arrays], core_ids=[0])
    return r.results[0]["out_0_dram"][:n]
```
